# Optimizing a Trainium2 kernel written in Bass

```python
import numpy as np
import jax
import jax.numpy as jnp

def _softmax(x, axis=-1):
    return jax.nn.softmax(x, axis=axis)

def _gelu(x):
    return jax.nn.gelu(x, approximate=True)

def _silu(x):
    return jax.nn.silu(x)

def _sigmoid(x):
    return jax.nn.sigmoid(x)

def _layernorm(x, axis=-1, eps=1e-05):
    m = jnp.mean(x, axis=axis, keepdims=True)
    v = jnp.var(x, axis=axis, keepdims=True)
    return (x - m) / jnp.sqrt(v + eps)

def _scatter_add(tgt, idx, src, axis=0):
    return tgt.at[idx].add(src)

def _segment_sum(src, seg, n):
    return jax.ops.segment_sum(src, seg, n)
kernel_name = 'mk_seq_preln_d2_jaxref_r8_1a0a92'

def setup_inputs(seed: int=0):
    np.random.seed(seed)
    _w = jnp.asarray

    def _L0_attn_setup():
        import jax, jax.numpy as jnp
        import numpy as np
        HIDDEN = 128
        D_MEM = 32
        BATCH = 4
        SEQ = 128
        EPS = 1e-06

        def elu_plus_one(x):
            return jnp.where(x > 0, x + 1.0, jnp.exp(x))

        def _retrieve(sigma_x, memory, memory_norm):
            a_unnorm = jnp.matmul(sigma_x, memory)
            norm = jnp.clip(jnp.matmul(sigma_x, memory_norm), EPS, None)[..., None]
            out = a_unnorm / norm
            return jnp.where(memory_norm.sum() < EPS, jnp.zeros_like(out), out)

        def _reference_tuple_inner(hidden_states, w_q, w_k, w_v, w_o, gate, memory, memory_norm):
            b, s, _ = hidden_states.shape
            q = jnp.einsum('bsh,dh->bsd', hidden_states, w_q)
            k = jnp.einsum('bsh,dh->bsd', hidden_states, w_k)
            v = jnp.einsum('bsh,dh->bsd', hidden_states, w_v)
            sigma_q = elu_plus_one(q)
            sigma_k = elu_plus_one(k)
            memory_output = _retrieve(sigma_q, memory, memory_norm)
            kv = jnp.einsum('bsd,bse->bsde', sigma_k, v)
            kv_cumsum = jnp.cumsum(kv, axis=1)
            k_cumsum = jnp.cumsum(sigma_k, axis=1)
            numerator = jnp.einsum('bsd,bsde->bse', sigma_q, kv_cumsum)
            denominator = jnp.clip(jnp.einsum('bsd,bsd->bs', sigma_q, k_cumsum), EPS, None)[..., None]
            local_output = numerator / denominator
            g = jax.nn.sigmoid(gate[0])
            combined = g * memory_output + (1.0 - g) * local_output
            output = jnp.einsum('bsd,hd->bsh', combined, w_o)
            retrieved_unnorm = jnp.matmul(sigma_k, memory)
            norm = jnp.clip(jnp.matmul(sigma_k, memory_norm), EPS, None)[..., None]
            delta_v = v - retrieved_unnorm / norm
            memory_update = jnp.einsum('bsd,bse->de', sigma_k, delta_v) / (b * s)
            new_memory = jax.lax.stop_gradient(memory + memory_update)
            z_update = sigma_k.sum(axis=(0, 1)) / b
            new_memory_norm = jax.lax.stop_gradient(memory_norm + z_update)
            return (output, new_memory, new_memory_norm)
        key = jax.random.key(seed)
        ks = jax.random.split(key, 8)
        hidden_states = jax.random.normal(ks[0], (BATCH, SEQ, HIDDEN), dtype=jnp.float32)
        s = 1.0 / np.sqrt(HIDDEN)
        w_q = jax.random.normal(ks[1], (D_MEM, HIDDEN), dtype=jnp.float32) * s
        w_k = jax.random.normal(ks[2], (D_MEM, HIDDEN), dtype=jnp.float32) * s
        w_v = jax.random.normal(ks[3], (D_MEM, HIDDEN), dtype=jnp.float32) * s
        w_o = jax.random.normal(ks[4], (HIDDEN, D_MEM), dtype=jnp.float32) * (1.0 / np.sqrt(D_MEM))
        gate = jnp.zeros((1,), dtype=jnp.float32)
        memory = jax.random.normal(ks[5], (D_MEM, D_MEM), dtype=jnp.float32) * 0.1
        memory_norm = jax.random.uniform(ks[6], (D_MEM,), dtype=jnp.float32) * 10.0 + 1.0
        return {'hidden_states': hidden_states, 'w_q': w_q, 'w_k': w_k, 'w_v': w_v, 'w_o': w_o, 'gate': gate, 'memory': memory, 'memory_norm': memory_norm}
    _L0_attn_in = _L0_attn_setup()

    def _L0_ffn_setup():
        import jax, jax.numpy as jnp
        import numpy as np
        NUM_EXPERTS = 160
        TOP_K = 8
        ROUTED_SCALE = 2.5
        HIDDEN = 128
        INTER = 64
        key = jax.random.key(seed)
        ks = jax.random.split(key, 7)
        B, S = (1, 256)
        return {'hidden_states': jax.random.normal(ks[0], (B, S, HIDDEN), dtype=jnp.float32), 'router_w': jax.random.normal(ks[1], (NUM_EXPERTS, HIDDEN), dtype=jnp.float32) * 0.02, 'expert_bias': jnp.zeros((NUM_EXPERTS,), dtype=jnp.float32), 'w_gate': jax.random.normal(ks[2], (NUM_EXPERTS, INTER, HIDDEN), dtype=jnp.float32) * 0.02, 'w_down': jax.random.normal(ks[3], (NUM_EXPERTS, HIDDEN, INTER), dtype=jnp.float32) * 0.02, 'w_gate_shared': jax.random.normal(ks[4], (INTER, HIDDEN), dtype=jnp.float32) * 0.02, 'w_down_shared': jax.random.normal(ks[5], (HIDDEN, INTER), dtype=jnp.float32) * 0.02}
    _L0_ffn_in = _L0_ffn_setup()

    def _L1_attn_setup():
        import jax, jax.numpy as jnp
        import numpy as np
        EMBED_DIM = 128
        NUM_HEADS = 16
        HEAD_DIM = EMBED_DIM // NUM_HEADS
        WINDOW_SIZE = 32
        HALF_BAND = 2 * WINDOW_SIZE
        BAND = 2 * HALF_BAND + 1
        key = jax.random.key(seed)
        ks = jax.random.split(key, 9)
        B, T, E = (1, 128, EMBED_DIM)
        scale = 0.02
        return {'hidden_states': jax.random.normal(ks[0], (B, T, E), jnp.float32), 'Wq': jax.random.normal(ks[1], (E, E), jnp.float32) * scale, 'bq': jax.random.normal(ks[2], (E,), jnp.float32) * scale, 'Wk': jax.random.normal(ks[3], (E, E), jnp.float32) * scale, 'bk': jax.random.normal(ks[4], (E,), jnp.float32) * scale, 'Wv': jax.random.normal(ks[5], (E, E), jnp.float32) * scale, 'bv': jax.random.normal(ks[6], (E,), jnp.float32) * scale, 'Wo': jax.random.normal(ks[7], (E, E), jnp.float32) * scale, 'bo': jax.random.normal(ks[8], (E,), jnp.float32) * scale}
    _L1_attn_in = _L1_attn_setup()

    def _L1_ffn_setup():
        import jax, jax.numpy as jnp
        import numpy as np
        B, N, D = (4, 256, 128)
        SPARSITY = 0.01
        key = jax.random.key(seed)
        k1, k2, k3 = jax.random.split(key, 3)
        x = jax.random.normal(k1, (B, N, D), dtype=jnp.float32)
        spatial = jax.random.normal(k2, (D, D), dtype=jnp.float32) * 0.02
        freq = jnp.fft.fft(spatial, axis=-1)
        k = int(D * SPARSITY)
        mag = jnp.abs(freq)
        kth = jax.lax.top_k(mag, k)[0][:, -1:]
        w_sparse = jnp.where(mag >= kth, freq, 0.0 + 0j)
        bias = jax.random.normal(k3, (D,), dtype=jnp.float32) * 0.01
        return {'x': x, 'w_freq_real': jnp.real(w_sparse).astype(jnp.float32), 'w_freq_imag': jnp.imag(w_sparse).astype(jnp.float32), 'bias': bias}
    _L1_ffn_in = _L1_ffn_setup()
    _d = {'L0_attn_hidden_states': _L0_attn_in['hidden_states'], 'L0_attn_w_q': _L0_attn_in['w_q'], 'L0_attn_w_k': _L0_attn_in['w_k'], 'L0_attn_w_v': _L0_attn_in['w_v'], 'L0_attn_w_o': _L0_attn_in['w_o'], 'L0_attn_gate': _L0_attn_in['gate'], 'L0_attn_memory': _L0_attn_in['memory'], 'L0_attn_memory_norm': _L0_attn_in['memory_norm'], 'L0_ffn_router_w': _L0_ffn_in['router_w'], 'L0_ffn_expert_bias': _L0_ffn_in['expert_bias'], 'L0_ffn_w_gate': _L0_ffn_in['w_gate'], 'L0_ffn_w_down': _L0_ffn_in['w_down'], 'L0_ffn_w_gate_shared': _L0_ffn_in['w_gate_shared'], 'L0_ffn_w_down_shared': _L0_ffn_in['w_down_shared'], 'L1_attn_Wq': _L1_attn_in['Wq'], 'L1_attn_bq': _L1_attn_in['bq'], 'L1_attn_Wk': _L1_attn_in['Wk'], 'L1_attn_bk': _L1_attn_in['bk'], 'L1_attn_Wv': _L1_attn_in['Wv'], 'L1_attn_bv': _L1_attn_in['bv'], 'L1_attn_Wo': _L1_attn_in['Wo'], 'L1_attn_bo': _L1_attn_in['bo'], 'L1_ffn_w_freq_real': _L1_ffn_in['w_freq_real'], 'L1_ffn_w_freq_imag': _L1_ffn_in['w_freq_imag'], 'L1_ffn_bias': _L1_ffn_in['bias']}
    _x0 = _d['L0_attn_hidden_states']
    _d['L0_attn_hidden_states'] = jax.random.normal(jax.random.fold_in(jax.random.key(seed), 1), (8, 512, 128), dtype=_x0.dtype)
    del _x0
    return _d

def reference(L0_attn_hidden_states, L0_attn_w_q, L0_attn_w_k, L0_attn_w_v, L0_attn_w_o, L0_attn_gate, L0_attn_memory, L0_attn_memory_norm, L0_ffn_router_w, L0_ffn_expert_bias, L0_ffn_w_gate, L0_ffn_w_down, L0_ffn_w_gate_shared, L0_ffn_w_down_shared, L1_attn_Wq, L1_attn_bq, L1_attn_Wk, L1_attn_bk, L1_attn_Wv, L1_attn_bv, L1_attn_Wo, L1_attn_bo, L1_ffn_w_freq_real, L1_ffn_w_freq_imag, L1_ffn_bias):

    def _L0_attn_ref(hidden_states, w_q, w_k, w_v, w_o, gate, memory, memory_norm):
        import jax, jax.numpy as jnp
        import numpy as np
        HIDDEN = 128
        D_MEM = 32
        BATCH = 4
        SEQ = 128
        EPS = 1e-06

        def elu_plus_one(x):
            return jnp.where(x > 0, x + 1.0, jnp.exp(x))

        def _retrieve(sigma_x, memory, memory_norm):
            a_unnorm = jnp.matmul(sigma_x, memory)
            norm = jnp.clip(jnp.matmul(sigma_x, memory_norm), EPS, None)[..., None]
            out = a_unnorm / norm
            return jnp.where(memory_norm.sum() < EPS, jnp.zeros_like(out), out)

        def _reference_tuple_inner(hidden_states, w_q, w_k, w_v, w_o, gate, memory, memory_norm):
            b, s, _ = hidden_states.shape
            q = jnp.einsum('bsh,dh->bsd', hidden_states, w_q)
            k = jnp.einsum('bsh,dh->bsd', hidden_states, w_k)
            v = jnp.einsum('bsh,dh->bsd', hidden_states, w_v)
            sigma_q = elu_plus_one(q)
            sigma_k = elu_plus_one(k)
            memory_output = _retrieve(sigma_q, memory, memory_norm)
            kv = jnp.einsum('bsd,bse->bsde', sigma_k, v)
            kv_cumsum = jnp.cumsum(kv, axis=1)
            k_cumsum = jnp.cumsum(sigma_k, axis=1)
            numerator = jnp.einsum('bsd,bsde->bse', sigma_q, kv_cumsum)
            denominator = jnp.clip(jnp.einsum('bsd,bsd->bs', sigma_q, k_cumsum), EPS, None)[..., None]
            local_output = numerator / denominator
            g = jax.nn.sigmoid(gate[0])
            combined = g * memory_output + (1.0 - g) * local_output
            output = jnp.einsum('bsd,hd->bsh', combined, w_o)
            retrieved_unnorm = jnp.matmul(sigma_k, memory)
            norm = jnp.clip(jnp.matmul(sigma_k, memory_norm), EPS, None)[..., None]
            delta_v = v - retrieved_unnorm / norm
            memory_update = jnp.einsum('bsd,bse->de', sigma_k, delta_v) / (b * s)
            new_memory = jax.lax.stop_gradient(memory + memory_update)
            z_update = sigma_k.sum(axis=(0, 1)) / b
            new_memory_norm = jax.lax.stop_gradient(memory_norm + z_update)
            return (output, new_memory, new_memory_norm)
        return _reference_tuple_inner(hidden_states, w_q, w_k, w_v, w_o, gate, memory, memory_norm)[0]

    def _L0_ffn_ref(hidden_states, router_w, expert_bias, w_gate, w_down, w_gate_shared, w_down_shared):
        import jax, jax.numpy as jnp
        import numpy as np
        NUM_EXPERTS = 160
        TOP_K = 8
        ROUTED_SCALE = 2.5
        HIDDEN = 128
        INTER = 64
        B, S, H = hidden_states.shape
        x = hidden_states.reshape(-1, H)
        T = x.shape[0]
        logits = x @ router_w.T + expert_bias[None, :]
        probs = jax.nn.sigmoid(logits)
        top_w, top_idx = jax.lax.top_k(probs, TOP_K)
        top_w = top_w / (jnp.sum(top_w, axis=-1, keepdims=True) + 1e-09)
        top_w = top_w * ROUTED_SCALE
        combine = jnp.zeros((T, NUM_EXPERTS), dtype=x.dtype)
        combine = combine.at[jnp.arange(T)[:, None], top_idx].set(top_w)
        h1 = jax.nn.silu(jnp.einsum('th,eih->eti', x, w_gate))
        h1w = h1 * combine.T[:, :, None]
        routed = jnp.einsum('eti,ehi->th', h1w, w_down)
        shared = jax.nn.silu(x @ w_gate_shared.T) @ w_down_shared.T
        return (routed + shared).reshape(B, S, H)

    def _L1_attn_ref(hidden_states, Wq, bq, Wk, bk, Wv, bv, Wo, bo):
        import jax, jax.numpy as jnp
        import numpy as np
        EMBED_DIM = 128
        NUM_HEADS = 16
        HEAD_DIM = EMBED_DIM // NUM_HEADS
        WINDOW_SIZE = 32
        HALF_BAND = 2 * WINDOW_SIZE
        BAND = 2 * HALF_BAND + 1
        B, T, E = hidden_states.shape
        H, D = (NUM_HEADS, HEAD_DIM)
        S = T
        q = hidden_states @ Wq.T + bq
        k = hidden_states @ Wk.T + bk
        v = hidden_states @ Wv.T + bv
        q = q.reshape(B, T, H, D).transpose(0, 2, 1, 3)
        k = k.reshape(B, S, H, D).transpose(0, 2, 1, 3)
        v = v.reshape(B, S, H, D).transpose(0, 2, 1, 3)
        offsets = jnp.arange(-HALF_BAND, HALF_BAND + 1)
        idx = jnp.arange(T)[:, None] + offsets[None, :]
        valid = (idx >= 0) & (idx < S)
        idxc = jnp.clip(idx, 0, S - 1)
        kb = k[:, :, idxc, :]
        vb = v[:, :, idxc, :]
        scaling = jnp.sqrt(jnp.asarray(D, jnp.float32))
        scores = jnp.einsum('bhtd,bhtwd->bhtw', q, kb) / scaling
        scores = jnp.where(valid[None, None], scores, -jnp.inf)
        probs = jax.nn.softmax(scores, axis=-1)
        ctx = jnp.einsum('bhtw,bhtwd->bhtd', probs, vb)
        ctx = ctx.transpose(0, 2, 1, 3).reshape(B, T, H * D)
        attn_output = ctx @ Wo.T + bo
        return attn_output

    def _L1_ffn_ref(x, w_freq_real, w_freq_imag, bias):
        import jax, jax.numpy as jnp
        import numpy as np
        B, N, D = (4, 256, 128)
        SPARSITY = 0.01
        w = jax.lax.complex(w_freq_real, w_freq_imag)
        x_freq = jnp.fft.fft(x, axis=-1)
        y_freq = jnp.einsum('bnd,do->bno', x_freq, w)
        y = jnp.real(jnp.fft.ifft(y_freq, axis=-1))
        return y + bias
    x = L0_attn_hidden_states
    x = x + _L0_attn_ref(_layernorm(x, axis=-1), L0_attn_w_q, L0_attn_w_k, L0_attn_w_v, L0_attn_w_o, L0_attn_gate, L0_attn_memory, L0_attn_memory_norm)
    x = x + _L0_ffn_ref(_layernorm(x, axis=-1), L0_ffn_router_w, L0_ffn_expert_bias, L0_ffn_w_gate, L0_ffn_w_down, L0_ffn_w_gate_shared, L0_ffn_w_down_shared)
    x = x + _L1_attn_ref(_layernorm(x, axis=-1), L1_attn_Wq, L1_attn_bq, L1_attn_Wk, L1_attn_bk, L1_attn_Wv, L1_attn_bv, L1_attn_Wo, L1_attn_bo)
    x = x + _L1_ffn_ref(_layernorm(x, axis=-1), L1_ffn_w_freq_real, L1_ffn_w_freq_imag, L1_ffn_bias)
    return x

_drawn_inputs = setup_inputs


def setup_inputs(seed=0):
    import zlib

    import numpy as np

    out = dict(_drawn_inputs(seed))
    spreads = {'L0_ffn_expert_bias': (0.0, 0.572)}
    factors = {'L0_attn_w_q': 8.0,
     'L0_attn_w_k': 5.657,
     'L0_attn_memory': 8.0,
     'L0_attn_memory_norm': 8.0,
     'L0_ffn_router_w': 3.644,
     'L0_ffn_w_gate': 3.48,
     'L0_ffn_w_down': 3.465,
     'L0_ffn_w_gate_shared': 3.092,
     'L0_ffn_w_down_shared': 3.05,
     'L1_attn_Wq': 8.0,
     'L1_attn_bq': 8.0,
     'L1_attn_Wk': 8.0,
     'L1_attn_bk': 8.0,
     'L1_attn_Wv': 8.0,
     'L1_attn_bv': 8.0,
     'L1_attn_Wo': 8.0,
     'L1_ffn_bias': 6.217}
    for name, (base, spread) in spreads.items():
        noise = np.random.default_rng([zlib.crc32(name.encode()), seed]).standard_normal(out[name].shape)
        drawn = base * np.exp(spread * noise) if base else spread * noise
        out[name] = jnp.asarray(drawn.astype(out[name].dtype))
    for name, factor in factors.items():
        out[name] = (out[name] * factor).astype(out[name].dtype)
    return out
```

```python
from contextlib import ExitStack

import numpy as np

import concourse.bass as bass
from concourse import mybir

F32 = mybir.dt.float32
BF16 = mybir.dt.bfloat16
ALU = mybir.AluOpType
ACT = mybir.ActivationFunctionType
AX = mybir.AxisListType

NB, SEQ, H = 8, 512, 128
P = 128
NT = SEQ // P
DM = 32
NE, INTER = 160, 64
NP = NE // 2
NJ = NP + 1
GE = 32
NG = NE // GE
PPG = GE // 2
NH, HD = 16, 8
HALF = 64
WIN = P + 2 * HALF
NU = NT * NH // 2
LN_EPS, EPS, GATE_EPS = 1e-5, 1e-6, 1e-9
ROUTED_SCALE = 2.5
SAT = 16.64
BIG = 1e30

PACK_A = [("ident", P), ("wq0", DM), ("wk0", DM), ("wv0", DM), ("causal", P), ("router", NE), ("ebias", 2 * NE),
          ("gate", 1), ("mhalf", NT), ("eps", NT), ("wo0", P), ("mem", DM), ("norm", 1), ("normrow", DM)]
PACK_B = [("wq", P), ("wk", P), ("wv", P), ("wo", P), ("band", WIN), ("bv", P), ("bo", P), ("fbias", P), ("bq", 1),
          ("bk", 1), ("headmask", 4), ("cos", P), ("sin", P), ("nsin", P), ("fr", P), ("fi", P), ("wgs", INTER),
          ("wds", P)]


def columns(pack):
    at, out = 0, {}
    for name, width in pack:
        out[name] = (at, at + width)
        at += width
    return out, at


COL_A, WIDTH_A = columns(PACK_A)
COL_B, WIDTH_B = columns(PACK_B)

Y_BACK, LN3_B, T3, QKV, V4, UNITS = 0, 2, 3, 4, 6, 7
POST = UNITS + NU + 3
PROJ, LN4_B, T4, FFN = POST + 1, POST + 3, POST + 4, POST + 5
LN1_A, LN1_B, T1, QKV0 = POST, POST + 2, POST + 3, POST + 6
CAUSAL, NUM, TCOMB, OPROJ = QKV0 + 4, QKV0 + 6, QKV0 + 8, QKV0 + 9
LN2_B, T2, ROUTER = OPROJ + 2, OPROJ + 3, OPROJ + 4
TOPK, GATES, CT = ROUTER + 1, ROUTER + 3, 79


def run_batches(eng, prologue, iteration, epilogue):
    prologue()
    iteration(0, False, True)
    with eng.Fori(1, NB - 1) as i:
        iteration(i, True, True)
    iteration(NB - 1, True, False)
    epilogue()


def window(t):
    lo, hi = max(0, P * t - HALF), min(SEQ, P * t + P + HALF)
    return lo, hi, lo - (P * t - HALF)


def chunk(t, c):
    if t == 0 and c == 0:
        return HALF, HALF
    return c * P, HALF if (t == NT - 1 and c == 1) else P


def chunk_tokens(m):
    return max(0, P * m - HALF), min(SEQ, P * m + HALF)


def build(nc, x, pack_a, pack_b, pack_c, w_up, w_down, out):
    with ExitStack() as ctx:
        def sb(name, shape, dt=F32):
            return ctx.enter_context(nc.sbuf_tensor(name, shape, dt))

        def sem(name):
            return ctx.enter_context(nc.semaphore(name))

        zp = ctx.enter_context(nc.psum_tensor("zp", [P, 2, SEQ], F32))
        gp = ctx.enter_context(nc.psum_tensor("gp", [P, 2, SEQ], F32))
        yp = ctx.enter_context(nc.psum_tensor("yp", [P, SEQ], F32))
        side = ctx.enter_context(nc.psum_tensor("side", [P, 3, SEQ], F32))

        pa = sb("pa", [P, WIDTH_A])
        pb = sb("pb", [P, WIDTH_B])
        pc = sb("pc", [P, PPG * P + P], BF16)
        a = {n: pa[:, lo:hi] for n, (lo, hi) in COL_A.items()}
        c = {n: pb[:, lo:hi] for n, (lo, hi) in COL_B.items()}
        spread = pc[:, 0:PPG * P]
        identb = pc[:, PPG * P:]
        wup = sb("wup", [P, NE * INTER])
        wdn = sb("wdn", [P, NP, P])

        sg_gate = sb("sg_gate", [P, 4])
        flag = sb("flag", [P, 2])
        memn = sb("memn", [DM, DM + 1])
        wds = sb("wds", [INTER, P])
        rT = sb("rT", [P, 2, P])
        ffn = sb("ffn", [P, P])

        x2Tn, x2Tc = sb("x2Tn", [P, SEQ]), sb("x2Tc", [P, SEQ])
        cTn, cTc = sb("cTn", [P, NG, SEQ], BF16), sb("cTc", [P, NG, SEQ], BF16)
        tb = sb("tb", [P, 2, SEQ])
        ub = sb("ub", [P, 3, SEQ])
        hb = sb("hb", [P, 3, SEQ])
        ysb = sb("ysb", [P, SEQ])

        stats = [sb(f"stats{n}", [P, NT, 6]) for n in range(4)]
        mv = [sb(f"mv{n}", [P, NT, 2]) for n in range(4)]
        ve = [sb(f"ve{n}", [P, NT]) for n in range(4)]
        rstd = [sb(f"rstd{n}", [P, NT]) for n in range(4)]
        xh01, xh23 = sb("xh01", [P, NT, P]), sb("xh23", [P, NT, P])
        xh = [xh01, xh01, xh23, xh23]

        xin = sb("xin", [P, NT, P])
        x1n, x1c = sb("x1n", [P, NT, P]), sb("x1c", [P, NT, P])
        xT = sb("xT", [P, SEQ])
        x1T = x3T = xT
        low, sg = sb("low", [DM, 2, SEQ]), sb("sg", [DM, 2, SEQ])
        elu = low
        va0 = sb("va0", [P, NT, DM + 1])
        at_cols = [0, SEQ, SEQ + 3 * P, SEQ + 5 * P, SEQ + 6 * P]
        qm = sb("qm", [P, 4, SEQ])
        AT = qm[:, :, :].rearrange("p a b -> p (a b)")
        dn, rc = sb("dn", [P, 8]), sb("rc", [P, 8])
        cmA, cmB, comb = sb("cmA", [P, NT, DM]), sb("cmB", [P, NT, DM]), sb("comb", [P, NT, DM])
        cbT = sb("cbT", [DM, SEQ])
        lg, key, rep, ex = (sb(n, [P, NT, NE]) for n in ("lg", "key", "rep", "ex"))
        sel = rep
        ex1 = prob = wt = cw = ex
        r1 = lg
        top = sb("top", [P, NT, 8])
        tot = sb("tot", [P, 4, NT])
        parts = sb("parts", [P, NT, NG, 3, GE], BF16)

        x2, x2b, x3, x3b = (sb(n, [P, NT, P]) for n in ("x2", "x2b", "x3", "x3b"))
        kT = sb("kT", [P, SEQ])
        va = sb("va", [P, NT + 1, NH, HD + 1])
        sm = sb("sm", [P, 2, 2, WIN])
        pr = sm
        mn = sb("mn", [P, 2, 2])
        pT = sb("pT", [P, 2, 4, P])
        rd = sb("rd", [P, NH])
        cx = sb("cx", [P, NT, P])
        cxT = sb("cxT", [P, SEQ])
        x4T = cxT
        osb = sb("osb", [P, NT, P])

        s_a, s_b, s_c, s_x, s_out = sem("s_a"), sem("s_b"), sem("s_c"), sem("s_x"), sem("s_out")
        s_w = [sem(f"s_w{g}") for g in range(NG)]
        s_gate, s_memn, s_rT, s_wds = sem("s_gate"), sem("s_memn"), sem("s_rT"), sem("s_wds")
        s_f1, s_f2, s_ffnw, s_ones = sem("s_f1"), sem("s_f2"), sem("s_ffnw"), sem("s_ones")
        s_z, s_t, s_u, s_g, s_h, s_y = (sem(n) for n in ("s_z", "s_t", "s_u", "s_g", "s_h", "s_y"))
        s_ysb, s_x2Tc, s_cTc, s_x1c = sem("s_ysb"), sem("s_x2Tc"), sem("s_cTc"), sem("s_x1c")
        s_var = [sem(f"s_var{n}") for n in range(4)]
        s_rstd = [sem(f"s_rstd{n}") for n in range(4)]
        s_xh = [sem(f"s_xh{n}") for n in range(4)]
        (f_T1, f_qk0, f_v0, f_num, f_Tcomb, f_oproj, f_T2, f_router, f_cT) = (
            sem(n) for n in ("f_T1", "f_qk0", "f_v0", "f_num", "f_Tcomb", "f_oproj", "f_T2", "f_router", "f_cT"))
        (f_Ty, f_T3, f_q, f_k, f_v, f_v4, f_Tctx, f_proj, f_T4, f_ffn) = (
            sem(n) for n in ("f_Ty", "f_T3", "f_q", "f_k", "f_v", "f_v4", "f_Tctx", "f_proj", "f_T4", "f_ffn"))
        (s_x1T, s_low, s_elu, s_sg, s_v0, s_comb, s_cbT, s_x1, s_x2T, s_lg, s_ex, s_prob, s_wt, s_sc,
         s_parts) = (sem(n) for n in (
             "s_x1T", "s_low", "s_elu", "s_sg", "s_v0", "s_comb", "s_cbT", "s_x1", "s_x2T", "s_lg", "s_ex",
             "s_prob", "s_wt", "s_sc", "s_parts"))
        (s_x2, s_x2b, s_x3T, s_qm, s_kT, s_v, s_v4, s_cxT, s_x3, s_x3b, s_x4T, s_o) = (sem(n) for n in (
            "s_x2", "s_x2b", "s_x3T", "s_qm", "s_kT", "s_v", "s_v4", "s_cxT", "s_x3", "s_x3b", "s_x4T", "s_o"))
        f_AT, s_ATd, s_ATc, s_cT = sem("f_AT"), sem("s_ATd"), sem("s_ATc"), sem("s_cT")
        f_sc, s_sm, s_pr, f_pT, s_pT = sem("f_sc"), sem("s_sm"), sem("s_pr"), sem("f_pT"), sem("s_pT")
        f_pv, s_cx = sem("f_pv"), sem("s_cx")

        xv = x.rearrange("b (t p) h -> b p t h", p=P)
        ov = out.rearrange("b (t p) h -> b p t h", p=P)
        block = ctx.enter_context(nc.Block())

        @block.sync
        def _(sp):
            def load_x(b):
                sp.wait_ge(s_x1, b)
                sp.dma_start(xin[:, :, :], xv[b]).then_inc(s_x, 16)

            load_x(0)
            sp.dma_start(pa[:, :], pack_a).then_inc(s_a, 16)
            sp.dma_start(pc[:, :], pack_c).then_inc(s_c, 16)
            for g in range(NG):
                sp.dma_start(wup[:, g * GE * INTER:(g + 1) * GE * INTER],
                             w_up[:, g * GE * INTER:(g + 1) * GE * INTER]).then_inc(s_w[g], 16)
                sp.dma_start(wdn[:, g * PPG:(g + 1) * PPG, :], w_down[:, g * PPG:(g + 1) * PPG, :]).then_inc(s_w[g], 16)
                if g == 0:
                    sp.dma_start(pb[:, :], pack_b).then_inc(s_b, 16)

            def iteration(i, before, after):
                if after:
                    load_x(i + 1)
                if before:
                    sp.wait_ge(s_o, i)
                    sp.dma_start(ov[i - 1], osb[:, :, :]).then_inc(s_out, 16)

            def epilogue():
                sp.wait_ge(s_o, NB)
                sp.dma_start(ov[NB - 1], osb[:, :, :]).then_inc(s_out, 16)
                sp.wait_ge(s_out, 16 * NB)

            run_batches(sp, lambda: None, iteration, epilogue)

        @block.tensor
        def _(pe):
            def transposes(bank, src):
                for t in range(NT):
                    last = pe.transpose(side[:, bank, t * P:(t + 1) * P], src(t), a["ident"])
                return last

            def setup():
                pe.wait_ge(s_b, 16)
                for k, (p1, p2, s2) in enumerate((("fr", "fi", "sin"), ("fi", "fr", "nsin"))):
                    pe.matmul(side[:, 1 + k, 0:P], c[p1], c["cos"], start=True, stop=False)
                    last = pe.matmul(side[:, 1 + k, 0:P], c[p2], c[s2], start=False, stop=True)
                last.then_inc(s_f1, 1)
                pe.wait_ge(s_rT, 1)
                pe.matmul(side[:, 1, 0:P], rT[:, 0, :], c["cos"], start=True, stop=False)
                pe.matmul(side[:, 1, 0:P], rT[:, 1, :], c["nsin"], start=False, stop=True).then_inc(s_f2, 1)
                pe.wait_ge(s_ffnw, 1)

            def l0_T1(b, before):
                pe.wait_ge(s_xh[0], b + 1)
                pe.wait_ge(s_cT, 3 * b)
                if before:
                    pe.wait_ge(s_cx, NT * (b - 1))
                transposes(2, lambda t: xh[0][:, t, :]).then_inc(f_T1, 1)

            def l0_qkv(b, before):
                pe.wait_ge(s_x1T, b + 1)
                if before:
                    pe.wait_ge(s_x4T, b - 1)
                    pe.wait_ge(s_o, b - 1)
                pe.matmul(side[0:DM, 0, :], a["wq0"], x1T[:, :], start=True, stop=True)
                pe.matmul(side[0:DM, 1, :], a["wk0"], x1T[:, :], start=True, stop=True).then_inc(f_qk0, 1)
                for t in range(NT):
                    last = pe.matmul(side[:, 2, t * DM:(t + 1) * DM], x1T[:, t * P:(t + 1) * P], a["wv0"],
                                     start=True, stop=True)
                last.then_inc(f_v0, 1)

            def l0_causal(b):
                pe.wait_ge(s_sg, b + 1)
                pe.wait_ge(s_v0, b + 1)
                for bank, kts in enumerate(((0,), (1,), (2, 3))):
                    for kt in kts:
                        at = at_cols[kt] - at_cols[kts[0]]
                        n = SEQ - kt * P
                        last = pe.matmul(side[:, bank, at:at + n], sg[:, 1, kt * P:(kt + 1) * P], sg[:, 0, kt * P:],
                                         start=True, stop=True)
                    last.then_inc(f_AT, 1)

            def l0_num(b):
                pe.wait_ge(s_ATc, 3 * b + 3)
                pe.wait_ge(s_ATd, 4 * b + 4)
                w = DM + 1
                for qt in range(NT):
                    for kt in range(qt + 1):
                        at = at_cols[kt] + (qt - kt) * P
                        pe.matmul(side[:, 0, qt * w:(qt + 1) * w], AT[:, at:at + P], va0[:, kt, :],
                                  start=(kt == 0), stop=(kt == qt))
                for qt in range(NT):
                    last = pe.matmul(side[:, 0, (NT + qt) * w:(NT + qt + 1) * w], sg[:, 0, qt * P:(qt + 1) * P],
                                     memn[:, :], start=True, stop=True)
                last.then_inc(f_num, 1)

            def l0_Tcomb(b):
                pe.wait_ge(s_comb, b + 1)
                for t in range(NT):
                    last = pe.transpose(side[0:DM, 1, t * P:(t + 1) * P], comb[:, t, :], a["ident"])
                last.then_inc(f_Tcomb, 1)

            def l0_oproj(b):
                pe.wait_ge(s_cbT, b + 1)
                for t in range(NT):
                    last = pe.matmul(side[:, 2, t * P:(t + 1) * P], cbT[:, t * P:(t + 1) * P], a["wo0"][0:DM],
                                     start=True, stop=True)
                last.then_inc(f_oproj, 1)

            def l0_T2(b):
                pe.wait_ge(s_xh[1], b + 1)
                transposes(0, lambda t: xh[1][:, t, :]).then_inc(f_T2, 1)

            def l0_router(b):
                pe.wait_ge(s_x2T, b + 1)
                for t in range(NT):
                    last = pe.matmul(side[:, 1 + t // 2, (t % 2) * NE:(t % 2 + 1) * NE], x2Tn[:, t * P:(t + 1) * P],
                                     a["router"], start=True, stop=True)
                last.then_inc(f_router, 1)

            def l0_cT(b):
                pe.wait_ge(s_parts, b + 1)
                pe.wait_ge(s_lg, b + 1)
                for g in range(NG):
                    bank = side[:, g // 2, :].bitcast(BF16)
                    for t in range(NT):
                        at = (g % 2) * SEQ + t * P
                        last = pe.transpose(bank[0:3 * GE, at:at + P],
                                            parts[:, t, g, :, :].rearrange("p k e -> p (k e)"), identb)
                    if g % 2 or g == NG - 1:
                        last.then_inc(f_cT, 1)

            def l1_Ty(b, gates):
                pe.wait_ge(s_ysb, b + 1)
                pe.wait_ge(s_cT, 3 * gates)
                if isinstance(b, int) and b == NB - 1:
                    pe.wait_ge(s_o, b)
                transposes(0, lambda t: ysb[:, t * P:(t + 1) * P]).then_inc(f_Ty, 1)

            def l1_T3(b):
                pe.wait_ge(s_xh[2], b + 1)
                transposes(1, lambda t: xh[2][:, t, :]).then_inc(f_T3, 1)

            def l1_qkv(b):
                pe.wait_ge(s_x3T, b + 1)
                pe.matmul(side[:, 0, :], c["wq"], x3T[:, :], start=True, stop=True).then_inc(f_q, 1)
                pe.matmul(side[:, 2, :], c["wk"], x3T[:, :], start=True, stop=True).then_inc(f_k, 1)
                for m in range(NT):
                    lo, hi = chunk_tokens(m)
                    last = pe.matmul(side[0:hi - lo, 1, m * P:(m + 1) * P], x3T[:, lo:hi], c["wv"],
                                     start=True, stop=True)
                last.then_inc(f_v, 1)

            def l1_v4(b):
                pe.wait_ge(s_kT, b + 1)
                lo, hi = chunk_tokens(NT)
                pe.matmul(side[0:hi - lo, 2, 0:P], x3T[:, lo:hi], c["wv"], start=True, stop=True).then_inc(f_v4, 1)

            def scores(b, w):
                t, hp = w // (NH // 2), w % (NH // 2)
                lo, hi, off = window(t)
                if w == 0:
                    pe.wait_ge(s_qm, b + 1)
                else:
                    pe.wait_ge(s_sm, NU * b + w)
                for k in range(2):
                    r, j = (2 * hp + k) // 4, (2 * hp + k) % 4
                    last = pe.matmul(side[:, 0, k * WIN + off:k * WIN + off + hi - lo],
                                     qm[32 * r:32 * r + 32, j, t * P:(t + 1) * P], kT[32 * r:32 * r + 32, lo:hi],
                                     start=True, stop=True)
                last.then_inc(f_sc, 1)

            def turn_probs(b, w):
                t = w // (NH // 2)
                pe.wait_ge(s_pr, NU * b + w + 1)
                if w == 0:
                    pe.wait_ge(s_v, b + 1)
                else:
                    pe.wait_ge(s_pT, NU * b + w)
                for k in range(2):
                    for cc in ((1, 0) if t == 0 else (0, 1)):
                        col, rows = chunk(t, cc)
                        last = pe.transpose(side[0:rows, 1, (2 * k + cc) * P:(2 * k + cc + 1) * P],
                                            pr[:, w % 2, k, col:col + rows], a["ident"])
                last.then_inc(f_pT, 1)

            def context(b, w):
                t, hp = w // (NH // 2), w % (NH // 2)
                pe.wait_ge(s_pT, NU * b + w + 1)
                if w == 0:
                    pe.wait_ge(s_v4, b + 1)
                elif hp == 0:
                    pe.wait_ge(s_cx, NT * b + t)
                for k in range(2):
                    h = 2 * hp + k
                    for cc in range(2):
                        _, rows = chunk(t, cc)
                        last = pe.matmul(side[:, 2, h * (HD + 1):(h + 1) * (HD + 1)], pT[0:rows, w % 2, 2 * k + cc, :],
                                         va[0:rows, t + cc, h, :], start=(cc == 0), stop=(cc == 1))
                if hp == NH // 2 - 1:
                    last.then_inc(f_pv, 1)

            def l1_Tctx(b):
                pe.wait_ge(s_cx, NT * b + NT)
                pe.wait_ge(s_sm, NU * b + NU)
                transposes(0, lambda t: cx[:, t, :]).then_inc(f_Tctx, 1)

            def project(f_sem, srcT, w):
                for t in range(NT):
                    last = pe.matmul(side[:, 1, t * P:(t + 1) * P], srcT[:, t * P:(t + 1) * P], w, start=True, stop=True)
                last.then_inc(f_sem, 1)

            def l1_proj(b):
                pe.wait_ge(s_cxT, b + 1)
                pe.wait_ge(s_pT, NU * b + NU)
                project(f_proj, cxT, c["wo"])

            def l1_T4(b):
                pe.wait_ge(s_xh[3], b + 1)
                transposes(0, lambda t: xh[3][:, t, :]).then_inc(f_T4, 1)

            def l1_ffn(b):
                pe.wait_ge(s_x4T, b + 1)
                pe.wait_ge(s_x3, b + 1)
                project(f_ffn, x4T, ffn[:, :])

            def up(i, j):
                if j == 0:
                    pe.wait_ge(s_x2Tc, i + 1)
                pe.wait_ge(s_u, NJ * i + max(0, j - 1))
                if j < NP:
                    pe.matmul(zp[:, j % 2, :], wup[:, j * P:(j + 1) * P], x2Tc[:, :], start=True, stop=True).then_inc(s_z, 1)
                else:
                    pe.matmul(zp[0:INTER, j % 2, :], c["wgs"], x2Tc[:, :], start=True, stop=True).then_inc(s_z, 1)

            def gates(i, j):
                if j == 0:
                    pe.wait_ge(s_cTc, i + 1)
                pe.wait_ge(s_h, NP * i + max(0, j - 1))
                g, u = j // PPG, j % PPG
                pe.matmul(gp[:, j % 2, :], spread[0:3 * GE, u * P:(u + 1) * P], cTc[0:3 * GE, g, :],
                          start=True, stop=True).then_inc(s_g, 1)

            def down(i, j):
                if j == 0:
                    pe.wait_ge(s_ysb, i)
                if j < NP:
                    pe.wait_ge(s_h, NP * i + j + 1)
                    pe.matmul(yp[:, :], wdn[:, j, :], hb[:, j % 3, :], start=(j == 0), stop=False).then_inc(s_y, 1)
                else:
                    pe.wait_ge(s_u, NJ * i + j + 1)
                    pe.matmul(yp[:, :], wds[:, :], ub[0:INTER, j % 3, :], start=False, stop=True).then_inc(s_y, 1)

            def banded(b, s, g):
                w = s - UNITS
                if s == Y_BACK:
                    l1_Ty(b, g)
                if s == T3:
                    l1_T3(b)
                if s == QKV:
                    l1_qkv(b)
                if s == V4:
                    l1_v4(b)
                if 0 <= w < NU:
                    scores(b, w)
                if 0 <= w - 1 < NU:
                    turn_probs(b, w - 1)
                if 0 <= w - 2 < NU:
                    context(b, w - 2)
                if s == POST:
                    l1_Tctx(b)
                if s == PROJ:
                    l1_proj(b)
                if s == T4:
                    l1_T4(b)
                if s == FFN:
                    l1_ffn(b)

            def linear(b, s, before):
                if s == T1:
                    l0_T1(b, before)
                if s == QKV0:
                    l0_qkv(b, before)
                if s == CAUSAL:
                    l0_causal(b)
                if s == NUM:
                    l0_num(b)
                if s == TCOMB:
                    l0_Tcomb(b)
                if s == OPROJ:
                    l0_oproj(b)
                if s == T2:
                    l0_T2(b)
                if s == ROUTER:
                    l0_router(b)
                if s == CT:
                    l0_cT(b)

            def iteration(i, before, after):
                for s in range(NJ + 2):
                    if s < NJ:
                        if s % PPG == 0 and isinstance(i, int) and i == 0 and s < NP:
                            pe.wait_ge(s_w[s // PPG], 32)
                        up(i, s)
                    if s < NP:
                        gates(i, s)
                    if before:
                        banded(i - 1, s, i + 1)
                    if after:
                        linear(i + 1, s, before)
                    if s >= 2:
                        down(i, s - 2)

            def prologue():
                pe.wait_ge(s_a, 16)
                pe.wait_ge(s_c, 16)
                setup()
                pe.wait_ge(s_memn, 1)
                pe.wait_ge(s_ones, 2)
                for s in range(NJ):
                    linear(0, s, False)
                pe.wait_ge(s_wds, 1)

            def epilogue():
                for s in range(NJ):
                    banded(NB - 1, s, NB)

            run_batches(pe, prologue, iteration, epilogue)

        @block.scalar
        def _(act):
            def setup():
                act.wait_ge(s_a, 16)
                act.activation(sg_gate[:, 0:1], a["gate"], ACT.Exp, scale=-1.0).then_inc(s_gate, 1)
                act.wait_ge(s_f1, 1)
                act.activation(rT[:, :, :], side[:, 1:3, 0:P], ACT.Copy).then_inc(s_rT, 1)
                act.wait_ge(s_f2, 1)
                act.activation(ffn[:, :], side[:, 1, 0:P], ACT.Copy, scale=1.0 / H).then_inc(s_ffnw, 1)

            def out_of_psum(dst, bank, full, value, done):
                act.wait_ge(full, value)
                act.activation(dst, side[:, bank, :], ACT.Copy).then_inc(done, 1)

            def linear(b, s):
                if s == T1:
                    out_of_psum(x1T[:, :], 2, f_T1, b + 1, s_x1T)
                if s == QKV0:
                    act.wait_ge(f_v0, b + 1)
                    act.activation(va0[:, :, 0:DM], side[:, 2, 0:NT * DM].rearrange("p (t e) -> p t e", t=NT),
                                   ACT.Copy).then_inc(s_v0, 1)
                if s == QKV0 + 1:
                    act.wait_ge(s_low, b + 1)
                    act.activation(elu[:, :, :], low[:, :, :], ACT.Exp).then_inc(s_elu, 1)
                if s == CAUSAL:
                    for bank, kt in enumerate((0, 1, 2)):
                        act.wait_ge(s_ATd, 4 * b + (1, 2, 4)[bank])
                        act.activation(AT[:, at_cols[kt] + P:at_cols[kt + 1]],
                                       side[:, bank, P:SEQ - kt * P], ACT.Copy).then_inc(s_ATc, 1)
                if s == TCOMB:
                    act.wait_ge(f_Tcomb, b + 1)
                    act.activation(cbT[:, :], side[0:DM, 1, :], ACT.Copy).then_inc(s_cbT, 1)
                if s == T2:
                    out_of_psum(x2Tn[:, :], 0, f_T2, b + 1, s_x2T)
                if s == TOPK:
                    act.wait_ge(s_lg, b + 1)
                    act.activation(ex[:, :, :], lg[:, :, :], ACT.Exp, scale=-1.0).then_inc(s_ex, 1)
                if s == CT:
                    act.wait_ge(s_cTc, b)
                    for k in range(3):
                        act.wait_ge(f_cT, 3 * b + k + 1)
                        n = 2 if k < 2 else 1
                        act.activation(cTn[0:3 * GE, 2 * k:2 * k + n, :].rearrange("p g t -> p (g t)"),
                                       side[0:3 * GE, k, :].bitcast(BF16)[:, 0:n * SEQ], ACT.Copy).then_inc(s_cT, 1)

            def banded(b, s):
                w = s - UNITS
                if s == T3:
                    out_of_psum(x3T[:, :], 1, f_T3, b + 1, s_x3T)
                if s == QKV:
                    act.wait_ge(f_k, b + 1)
                    act.activation(kT[:, :], side[:, 2, :], ACT.Identity, bias=c["bk"]).then_inc(s_kT, 1)
                if 0 <= w < NU:
                    exps(b, w)
                if 0 <= w - 1 < NU:
                    probs(b, w - 1)
                if s == POST:
                    out_of_psum(cxT[:, :], 0, f_Tctx, b + 1, s_cxT)
                if s == T4:
                    out_of_psum(x4T[:, :], 0, f_T4, b + 1, s_x4T)

            def exps(b, w):
                lo, hi, off = window(w // (NH // 2))
                act.wait_ge(s_sm, NU * b + w + 1)
                for k in range(2):
                    last = act.activation(pr[:, w % 2, k, off:off + hi - lo], sm[:, w % 2, k, off:off + hi - lo],
                                          ACT.Exp, scale=-1.0, bias=mn[:, w % 2, k:k + 1])
                last.then_inc(s_pr, 1)

            def probs(b, w):
                t = w // (NH // 2)
                act.wait_ge(f_pT, NU * b + w + 1)
                src = side[:, 1, :].rearrange("p (k q) -> p k q", k=4)
                if 0 < t < NT - 1:
                    act.activation(pT[:, w % 2, :, :], src, ACT.Copy).then_inc(s_pT, 1)
                    return
                for cc in range(2):
                    _, rows = chunk(t, cc)
                    last = act.activation(pT[0:rows, w % 2, cc::2, :], src[0:rows, cc::2, :], ACT.Copy)
                last.then_inc(s_pT, 1)

            def iteration(i, before, after):
                for s in range(NJ):
                    if s == 0:
                        if before:
                            act.wait_ge(s_z, NJ * i)
                        act.wait_ge(s_x2T, i + 1)
                        act.activation(x2Tc[:, :], x2Tn[:, :], ACT.Copy).then_inc(s_x2Tc, 1)
                        if before:
                            act.wait_ge(s_y, NJ * i)
                            act.activation(ysb[:, :], yp[:, :], ACT.Copy).then_inc(s_ysb, 1)
                    n = P if s < NP else INTER
                    act.wait_ge(s_z, NJ * i + s + 1)
                    act.wait_ge(s_u, NJ * i + max(0, s - 1))
                    act.activation(tb[0:n, s % 2, :], zp[0:n, s % 2, :], ACT.Tanh, scale=0.5).then_inc(s_t, 1)
                    if s == Y_BACK + 1:
                        act.wait_ge(s_x2, i)
                        act.wait_ge(s_x1, i + 1)
                        act.activation(x1c[:, :, :], x1n[:, :, :], ACT.Copy).then_inc(s_x1c, 1)
                    if before:
                        banded(i - 1, s)
                    if after:
                        linear(i + 1, s)

            def prologue():
                setup()
                for s in range(NJ):
                    linear(0, s)

            def epilogue():
                act.wait_ge(s_y, NJ * NB)
                act.activation(ysb[:, :], yp[:, :], ACT.Copy).then_inc(s_ysb, 1)
                for s in range(NJ):
                    banded(NB - 1, s)

            run_batches(act, prologue, iteration, epilogue)

        @block.vector
        def _(dve):
            def link(ins, wait=True):
                if wait:
                    dve.drain()

            def setup():
                dve.memset(va0[:, :, DM:DM + 1], 1.0).then_inc(s_ones, 1)
                dve.memset(va[:, :, :, HD:HD + 1], 1.0).then_inc(s_ones, 1)
                dve.wait_ge(s_a, 16)
                dve.wait_ge(s_gate, 1)
                link(dve.tensor_scalar(sg_gate[:, 1:2], sg_gate[:, 0:1], 1.0, None, ALU.add))
                link(dve.reciprocal(sg_gate[:, 2:3], sg_gate[:, 1:2]))
                link(dve.tensor_scalar(sg_gate[:, 3:4], sg_gate[:, 2:3], -1.0, 1.0, ALU.mult, ALU.add))
                link(dve.tensor_reduce(flag[:, 0:1], a["normrow"], AX.X, ALU.add))
                link(dve.tensor_scalar(flag[:, 1:2], flag[:, 0:1], EPS, None, ALU.is_ge))
                link(dve.tensor_scalar(memn[:, 0:DM], a["mem"][0:DM], sg_gate[0:DM, 2:3], flag[0:DM, 1:2],
                                       ALU.mult, ALU.mult))
                dve.tensor_copy(memn[:, DM:DM + 1], a["norm"][0:DM]).then_inc(s_memn, 1)

            def late_setup():
                dve.wait_ge(s_b, 16)
                dve.tensor_scalar(wds[:, :], c["wds"][0:INTER], 0.5, None, ALU.mult).then_inc(s_wds, 1)

            def norm_stats(n, src, b):
                for t in range(NT):
                    link(dve.bn_stats(stats[n][:, t, :], src[:, t, :]), wait=(t == NT - 1))
                for t in range(NT):
                    last = dve.bn_aggr(mv[n][:, t, :], stats[n][:, t, :])
                last.then_inc(s_var[n], 1)

            def norm_apply(n, src, b):
                dve.wait_ge(s_rstd[n], b + 1)
                for t in range(NT):
                    last = dve.tensor_scalar(xh[n][:, t, :], src[:, t, :], mv[n][:, t, 0:1], rstd[n][:, t:t + 1],
                                             ALU.subtract, ALU.mult)
                last.then_inc(s_xh[n], 1)

            def tiles(ap):
                return ap.rearrange("p (t e) -> p t e", t=NT)

            def linear(b, s):
                if s == LN1_A:
                    dve.wait_ge(s_x, 16 * b + 16)
                    norm_stats(0, xin, b)
                if s == LN1_B:
                    norm_apply(0, xin, b)
                if s == QKV0:
                    dve.wait_ge(f_qk0, b + 1)
                    dve.tensor_scalar(low[:, :, :], side[0:DM, 0:2, :], 0.0, None, ALU.min).then_inc(s_low, 1)
                if s == QKV0 + 2:
                    dve.wait_ge(s_elu, b + 1)
                    dve.scalar_tensor_tensor(sg[:, :, :], side[0:DM, 0:2, :], 0.0, elu[:, :, :], ALU.max,
                                             ALU.add).then_inc(s_sg, 1)
                if s == CAUSAL:
                    for bank, kt in ((0, 0), (1, 1), (2, 2), (2, 3)):
                        dve.wait_ge(f_AT, 3 * b + bank + 1)
                        at = 2 * P if kt == 3 else 0
                        dve.tensor_tensor(AT[:, at_cols[kt]:at_cols[kt] + P], side[:, bank, at:at + P], a["causal"],
                                          ALU.mult).then_inc(s_ATd, 1)
                if s == NUM:
                    dve.wait_ge(f_num, b + 1)
                    v = side[:, 0, 0:8 * (DM + 1)].rearrange("p (m e) -> p m e", m=8)
                    link(dve.tensor_scalar(dn[:, :].unsqueeze(2), v[:, :, DM:DM + 1], EPS, None, ALU.max))
                    link(dve.reciprocal(rc[:, :], dn[:, :]))
                    link(dve.tensor_scalar(rc[:, 0:NT], rc[:, 0:NT], sg_gate[:, 3:4], None, ALU.mult))
                    for dst, lo in ((cmA, 0), (cmB, NT)):
                        link(dve.tensor_tensor(dst[:, :, :], v[:, lo:lo + NT, 0:DM],
                                               rc[:, lo:lo + NT].unsqueeze(2).to_broadcast([P, NT, DM]), ALU.mult),
                             wait=(lo == NT))
                    dve.tensor_tensor(comb[:, :, :], cmA[:, :, :], cmB[:, :, :], ALU.add).then_inc(s_comb, 1)
                if s == OPROJ:
                    dve.wait_ge(f_oproj, b + 1)
                    dve.wait_ge(s_x1c, b)
                    dve.tensor_tensor(x1n[:, :, :], tiles(side[:, 2, :]), xin[:, :, :], ALU.add).then_inc(s_x1, 1)
                    dve.wait_ge(s_x1, b + 1)
                    norm_stats(1, x1n, b)
                if s == LN2_B:
                    norm_apply(1, x1n, b)
                if s == ROUTER:
                    dve.wait_ge(f_router, b + 1)
                    dve.tensor_tensor(lg[:, :, :].rearrange("p (u v) e -> p u (v e)", u=2), side[:, 1:3, 0:2 * NE],
                                      a["ebias"].unsqueeze(1).to_broadcast([P, 2, 2 * NE]), ALU.add).then_inc(s_lg, 1)
                    dve.wait_ge(s_lg, b + 1)
                    link(dve.tensor_scalar(key[:, :, :], lg[:, :, :], SAT, -87.0, ALU.min, ALU.max))
                if s == TOPK:
                    for t in range(NT):
                        link(dve.max(top[:, t, :], key[:, t, :]), wait=(t == NT - 1))
                    for t in range(NT):
                        link(dve.match_replace(rep[:, t, :], top[:, t, :], key[:, t, :], -BIG), wait=(t == NT - 1))
                if s == TOPK + 1:
                    dve.wait_ge(s_ex, b + 1)
                    dve.tensor_scalar(ex1[:, :, :], ex[:, :, :], 1.0, None, ALU.add)
                    link(dve.tensor_tensor(sel[:, :, :], rep[:, :, :], key[:, :, :], ALU.not_equal))
                    dve.reciprocal(prob[:, :, :], ex1[:, :, :]).then_inc(s_prob, 1)
                if s == GATES:
                    dve.wait_ge(s_wt, b + 1)
                    link(dve.tensor_reduce(tot[:, 0, :], wt[:, :, :], AX.X, ALU.add))
                    link(dve.tensor_scalar(tot[:, 1, :], tot[:, 0, :], GATE_EPS, None, ALU.add))
                    link(dve.reciprocal(tot[:, 2, :], tot[:, 1, :]))
                    dve.tensor_scalar(tot[:, 3, :], tot[:, 2, :], ROUTED_SCALE / 2, None, ALU.mult).then_inc(s_sc, 1)

            def banded(b, s):
                w = s - UNITS
                if s == Y_BACK:
                    dve.wait_ge(f_Ty, b + 1)
                    dve.wait_ge(s_x1c, b + 1)
                    dve.tensor_tensor(x2[:, :, :], tiles(side[:, 0, :]), x1c[:, :, :], ALU.add).then_inc(s_x2, 1)
                    dve.wait_ge(s_x2, b + 1)
                    norm_stats(2, x2, b)
                if s == LN3_B:
                    norm_apply(2, x2, b)
                if s == QKV:
                    dve.wait_ge(f_q, b + 1)
                    for j in range(4):
                        last = dve.tensor_scalar(qm[:, j, :], side[:, 0, :], c["bq"], c["headmask"][:, j:j + 1],
                                                 ALU.add, ALU.mult)
                    last.then_inc(s_qm, 1)
                if s == QKV + 1:
                    dve.wait_ge(f_v, b + 1)
                    for m in range(NT):
                        last = values(m, 1, m * P)
                    last.then_inc(s_v, 1)
                if s == V4:
                    dve.wait_ge(f_v4, b + 1)
                    values(NT, 2, 0).then_inc(s_v4, 1)
                if 0 <= w < NU:
                    masked(b, w)
                if w >= 2 and (w - 2) % (NH // 2) == NH // 2 - 1 and w - 2 < NU:
                    t = (w - 2) // (NH // 2)
                    dve.wait_ge(f_pv, NT * b + t + 1)
                    v = side[:, 2, 0:NH * (HD + 1)].rearrange("p (h e) -> p h e", h=NH)
                    link(dve.reciprocal(rd[:, :].unsqueeze(2), v[:, :, HD:HD + 1]))
                    dve.tensor_tensor(cx[:, t, :].rearrange("p (h e) -> p h e", h=NH), v[:, :, 0:HD],
                                      rd[:, :].unsqueeze(2).to_broadcast([P, NH, HD]), ALU.mult).then_inc(s_cx, 1)
                if s == PROJ:
                    dve.wait_ge(f_proj, b + 1)
                    dve.wait_ge(s_x2b, b + 1)
                    dve.tensor_tensor(x3[:, :, :], tiles(side[:, 1, :]), x2b[:, :, :], ALU.add).then_inc(s_x3, 1)
                    dve.wait_ge(s_x3, b + 1)
                    norm_stats(3, x3, b)
                if s == LN4_B:
                    norm_apply(3, x3, b)
                if s == FFN:
                    dve.wait_ge(f_ffn, b + 1)
                    dve.wait_ge(s_x3b, b + 1)
                    dve.tensor_tensor(osb[:, :, :], tiles(side[:, 1, :]), x3b[:, :, :], ALU.add).then_inc(s_o, 1)

            def values(m, bank, at):
                lo, hi = chunk_tokens(m)
                n = hi - lo
                return dve.tensor_tensor(va[0:n, m, :, 0:HD],
                                         side[0:n, bank, at:at + P].rearrange("p (h e) -> p h e", h=NH),
                                         c["bv"][0:n].rearrange("p (h e) -> p h e", h=NH), ALU.add)

            def wait_scores(b, w):
                dve.wait_ge(f_sc, NU * b + w + 1)
                if w >= 2:
                    dve.wait_ge(f_pT, NU * b + w - 1)

            def masked(b, w):
                lo, hi, off = window(w // (NH // 2))
                n = hi - lo
                for k in range(2):
                    last = dve.tensor_tensor_reduce(sm[:, w % 2, k, off:off + n],
                                                    side[:, 0, k * WIN + off:k * WIN + off + n],
                                                    c["band"][:, off:off + n], 1.0, 3e38, ALU.add, ALU.min,
                                                    mn[:, w % 2, k:k + 1])
                last.then_inc(s_sm, 1)

            def gated(i, j):
                dve.wait_ge(s_g, NP * i + j + 1)
                dve.wait_ge(s_u, NJ * i + j + 1)
                if j >= 3:
                    dve.wait_ge(s_y, NJ * i + j - 2)
                dve.tensor_tensor(hb[:, j % 3, :], gp[:, j % 2, :], ub[:, j % 3, :], ALU.mult).then_inc(s_h, 1)

            def iteration(i, before, after):
                for s in range(NJ + 1):
                    if s == 0:
                        dve.wait_ge(s_cT, 3 * i + 3)
                        dve.wait_ge(s_g, NP * i)
                        dve.tensor_copy(cTc[0:3 * GE, :, :], cTn[0:3 * GE, :, :]).then_inc(s_cTc, 1)
                    if s < NJ:
                        n = P if s < NP else INTER
                        dve.wait_ge(s_t, NJ * i + s + 1)
                        if s == 0:
                            dve.wait_ge(s_y, NJ * i)
                        dve.wait_ge(s_h, NP * i + max(0, s - 2))
                        dve.scalar_tensor_tensor(ub[0:n, s % 3, :], tb[0:n, s % 2, :], 1.0, zp[0:n, s % 2, :],
                                                 ALU.add, ALU.mult).then_inc(s_u, 1)
                    if before and 0 <= s - UNITS < NU:
                        wait_scores(i - 1, s - UNITS)
                    if 1 <= s <= NP:
                        gated(i, s - 1)
                    if before and s < NJ:
                        banded(i - 1, s)
                    if after and s < NJ:
                        linear(i + 1, s)

                if before:
                    dve.wait_ge(s_out, 16 * i)

            def prologue():
                setup()
                for s in range(NJ):
                    linear(0, s)
                late_setup()

            def epilogue():
                for s in range(NJ):
                    if 0 <= s - UNITS < NU:
                        wait_scores(NB - 1, s - UNITS)
                    banded(NB - 1, s)

            run_batches(dve, prologue, iteration, epilogue)

        @block.gpsimd
        def _(pool):
            def inverse_root(n, b):
                pool.wait_ge(s_var[n], b + 1)
                pool.tensor_tensor(ve[n][:, :].unsqueeze(2), mv[n][:, :, 1:2], a["eps"].unsqueeze(2), ALU.add)
                pool.drain()
                pool.tensor_tensor(rstd[n][:, :], ve[n][:, :], a["mhalf"], ALU.pow).then_inc(s_rstd[n], 1)

            def linear(b, s):
                if s == LN1_A:
                    inverse_root(0, b)
                if s == OPROJ:
                    inverse_root(1, b)
                if s == TOPK + 1:
                    pool.wait_ge(s_prob, b + 1)
                    pool.tensor_tensor(wt[:, :, :], prob[:, :, :], sel[:, :, :], ALU.mult).then_inc(s_wt, 1)
                if s == GATES:
                    pool.wait_ge(s_sc, b + 1)
                    pool.tensor_tensor(cw[:, :, :], wt[:, :, :], tot[:, 3, :].unsqueeze(2).to_broadcast([P, NT, NE]),
                                       ALU.mult)
                    pool.drain()
                    grouped = lambda v: v[:, :, :].rearrange("p t (g e) -> p t g e", g=NG)
                    pool.tensor_copy(parts[:, :, :, 0, :], grouped(cw))
                    pool.drain()
                    pool.tensor_tensor(grouped(r1), grouped(cw), parts[:, :, :, 0, :], ALU.subtract)
                    pool.drain()
                    pool.tensor_copy(parts[:, :, :, 1, :], grouped(r1))
                    pool.drain()
                    pool.tensor_tensor(parts[:, :, :, 2, :], grouped(r1), parts[:, :, :, 1, :],
                                       ALU.subtract).then_inc(s_parts, 1)

            def banded(b, s):
                bias = lambda n: c[n].unsqueeze(1).to_broadcast([P, NT, P])
                if s == Y_BACK:
                    inverse_root(2, b)
                    pool.tensor_tensor(x2b[:, :, :], x2[:, :, :], bias("bo"), ALU.add).then_inc(s_x2b, 1)
                if s == PROJ:
                    inverse_root(3, b)
                    pool.tensor_tensor(x3b[:, :, :], x3[:, :, :], bias("fbias"), ALU.add).then_inc(s_x3b, 1)

            def iteration(i, before, after):
                for s in range(NJ):
                    if before:
                        banded(i - 1, s)
                    if after:
                        linear(i + 1, s)

            def prologue():
                pool.wait_ge(s_a, 16)
                for s in range(NJ):
                    linear(0, s)
                pool.wait_ge(s_b, 16)

            def epilogue():
                for s in range(NJ):
                    banded(NB - 1, s)

            run_batches(pool, prologue, iteration, epilogue)


def packed(pack, parts):
    cols, width = columns(pack)
    out = np.zeros((P, width), np.float32)
    for name, (lo, hi) in cols.items():
        out[:parts[name].shape[0], lo:hi] = parts[name]
    return out


def shape_constants():
    k = np.arange(P)
    angle = 2 * np.pi * ((k[:, None] * k[None, :]) % P) / P
    col = np.arange(WIN)
    part = (k % 32) // HD
    spread = np.zeros((P, PPG * P), np.float32)
    for row in range(3 * GE):
        for_expert = row % GE
        spread[row, for_expert * INTER:(for_expert + 1) * INTER] = 1.0
    return {
        "ident": np.eye(P), "causal": (k[None, :] >= k[:, None]).astype(np.float32), "mhalf": np.full((P, NT), -0.5),
        "eps": np.full((P, NT), LN_EPS),
        "band": np.where((col[None, :] >= k[:, None]) & (col[None, :] <= k[:, None] + 2 * HALF), 0.0, BIG),
        "headmask": np.where(part[:, None] == np.arange(4)[None, :], -1.0 / np.sqrt(HD), 0.0),
        "cos": np.cos(angle), "sin": np.sin(angle), "nsin": -np.sin(angle),
    }, spread


def kernel(L0_attn_hidden_states, L0_attn_w_q, L0_attn_w_k, L0_attn_w_v, L0_attn_w_o, L0_attn_gate, L0_attn_memory,
           L0_attn_memory_norm, L0_ffn_router_w, L0_ffn_expert_bias, L0_ffn_w_gate, L0_ffn_w_down,
           L0_ffn_w_gate_shared, L0_ffn_w_down_shared, L1_attn_Wq, L1_attn_bq, L1_attn_Wk, L1_attn_bk, L1_attn_Wv,
           L1_attn_bv, L1_attn_Wo, L1_attn_bo, L1_ffn_w_freq_real, L1_ffn_w_freq_imag, L1_ffn_bias):
    import ml_dtypes
    import concourse.bacc as bacc
    from concourse.bass_utils import run_bass_kernel_spmd

    const, spread = shape_constants()
    rows = lambda v, n=P: np.broadcast_to(np.asarray(v)[None, :], (n, np.asarray(v).shape[0]))
    T = lambda v: np.asarray(v).T
    col = lambda v: np.asarray(v)[:, None]
    bias2 = np.concatenate([np.asarray(L0_ffn_expert_bias)] * 2)
    in_a = packed(PACK_A, {
        **const, "wq0": T(L0_attn_w_q), "wk0": T(L0_attn_w_k), "wv0": T(L0_attn_w_v), "router": T(L0_ffn_router_w),
        "ebias": rows(bias2), "gate": rows(L0_attn_gate), "wo0": T(L0_attn_w_o), "mem": np.asarray(L0_attn_memory),
        "norm": col(L0_attn_memory_norm), "normrow": rows(L0_attn_memory_norm)})
    in_b = packed(PACK_B, {
        **const, "wq": T(L1_attn_Wq), "wk": T(L1_attn_Wk), "wv": T(L1_attn_Wv), "wo": T(L1_attn_Wo),
        "bv": rows(L1_attn_bv), "bo": rows(L1_attn_bo), "fbias": rows(L1_ffn_bias), "bq": col(L1_attn_bq),
        "bk": col(L1_attn_bk), "fr": np.asarray(L1_ffn_w_freq_real), "fi": np.asarray(L1_ffn_w_freq_imag),
        "wgs": T(L0_ffn_w_gate_shared), "wds": T(L0_ffn_w_down_shared)})
    in_c = np.concatenate([spread, np.eye(P, dtype=np.float32)], axis=1).astype(ml_dtypes.bfloat16)
    up = np.ascontiguousarray(np.asarray(L0_ffn_w_gate).transpose(2, 0, 1).reshape(H, NE * INTER))
    down = np.ascontiguousarray(
        np.asarray(L0_ffn_w_down).reshape(NP, 2, H, INTER).transpose(1, 3, 0, 2).reshape(P, NP, H))

    nc = bacc.Bacc("TRN2", target_bir_lowering=False, num_devices=1)
    arrays = {"in_x": np.ascontiguousarray(L0_attn_hidden_states), "in_a": in_a, "in_b": in_b, "in_c": in_c,
              "in_up": up, "in_down": down}
    aps = [nc.dram_tensor(n, v.shape, mybir.dt.from_np(v.dtype), kind="ExternalInput").ap() for n, v in arrays.items()]
    out = nc.dram_tensor("out_y", (NB, SEQ, H), F32, kind="ExternalOutput").ap()
    build(nc, *aps, out)
    r = run_bass_kernel_spmd(nc, [arrays], core_ids=[0])
    return r.results[0]["out_y"]
```

```python
from contextlib import ExitStack

import numpy as np

import concourse.bass as bass
from concourse import mybir

F32 = mybir.dt.float32
F16 = mybir.dt.float16
ALU = mybir.AluOpType
ACT = mybir.ActivationFunctionType
AX = mybir.AxisListType

NB, SEQ, H = 8, 512, 128
P = 128
NT = SEQ // P
DM = 32
NE, INTER = 160, 64
NP = NE // 2
NJ = NP + 1
GE = 40
NG = NE // GE
PPG = GE // 2
NH, HD = 16, 8
HALF = 64
WIN = P + 2 * HALF
PS = 2.0 ** 15
VW = 2 * (HD + 1)
NU = NT * NH // 2
LN_EPS, EPS, GATE_EPS = 1e-5, 1e-6, 1e-9
ROUTED_SCALE = 2.5
SAT = 16.64
BIG = 1e30
WS = 16.0
GS = 1024.0
CH = 8
NCH = NP // CH

PACK_A = [("ident", P), ("wq0", DM), ("wk0", DM), ("wv0", DM), ("causal", P), ("router", NE), ("ebias", 2 * NE),
          ("gate", 1), ("mhalf", NT), ("eps", NT), ("wo0", P), ("mem", DM), ("norm", 1), ("normrow", DM)]
PACK_B = [("wqk", 8 * P), ("wv", P), ("wo", P), ("band", WIN), ("bv", P), ("bo", P), ("fbias", P), ("bqk", 8),
          ("rest", 2), ("wgs", INTER), ("wds", P)]
PACK_D = [("cos", P), ("sin", P), ("nsin", P), ("fr", P), ("fi", P)]


def columns(pack):
    at, out = 0, {}
    for name, width in pack:
        out[name] = (at, at + width)
        at += width
    return out, at


COL_A, WIDTH_A = columns(PACK_A)
COL_B, WIDTH_B = columns(PACK_B)
COL_D, WIDTH_D = columns(PACK_D)

Y_BACK = 4
LN3_B, T3, QKV = Y_BACK + 2, Y_BACK + 3, Y_BACK + 4
UNITS = QKV + 4
POST = UNITS + NU + 6
PROJ, LN4_B, T4, FFN = POST + 1, POST + 3, POST + 4, POST + 5
LN1_A, LN1_B, T1, QKV0 = POST - 9, POST - 7, POST, POST + 7
CAUSAL, NUM, TCOMB, OPROJ = QKV0 + 3, QKV0 + 5, QKV0 + 6, QKV0 + 7
LN2_B, T2, ROUTER = OPROJ + 2, OPROJ + 3, OPROJ + 4
GATES = ROUTER + 6
CT = GATES + 5
assert CT < NJ - 1 and NJ % 3 == 0


def run_batches(eng, prologue, iteration, epilogue):
    prologue()
    iteration(0, 0, False, True)
    with eng.Fori(0, NB // 2 - 1) as turn:
        iteration(2 * turn + 1, 1, True, True)
        iteration(2 * turn + 2, 0, True, True)
    iteration(NB - 1, 1, True, False)
    epilogue()


def window(t):
    lo, hi = max(0, P * t - HALF), min(SEQ, P * t + P + HALF)
    return lo, hi, lo - (P * t - HALF)


def chunk(t, c):
    if t == 0 and c == 0:
        return HALF, HALF
    return c * P, HALF if (t == NT - 1 and c == 1) else P


def chunk_tokens(m):
    return max(0, P * m - HALF), min(SEQ, P * m + HALF)


def heads(w):
    hp = w % (NH // 2)
    return [(4 * g + hp % 4, g, hp % 4) for g in (2 * (hp // 4), 2 * (hp // 4) + 1)]


def build(nc, x, pack_a, pack_b, pack_c, pack_d, w_up, w_down, out):
    with ExitStack() as ctx:
        def sb(name, shape, dt=F32):
            return ctx.enter_context(nc.sbuf_tensor(name, shape, dt))

        def sem(name):
            return ctx.enter_context(nc.semaphore(name))

        zp = ctx.enter_context(nc.psum_tensor("zp", [P, 2, SEQ], F32))
        gp = ctx.enter_context(nc.psum_tensor("gp", [P, 2, SEQ], F32))
        yp = ctx.enter_context(nc.psum_tensor("yp", [P, SEQ], F32))
        side = ctx.enter_context(nc.psum_tensor("side", [P, 3, SEQ], F32))

        pa = sb("pa", [P, WIDTH_A])
        pb = sb("pb", [P, WIDTH_B])
        pc = sb("pc", [P, PPG * P + P], F16)
        a = {n: pa[:, lo:hi] for n, (lo, hi) in COL_A.items()}
        c = {n: pb[:, lo:hi] for n, (lo, hi) in COL_B.items()}
        spread = pc[:, 0:PPG * P]
        identh = pc[:, PPG * P:]
        wup = sb("wup", [P, 2, NP, P], F16)
        wdn = sb("wdn", [P, 2, NP, P], F16)
        wgs, wds = sb("wgs", [P, 2, INTER], F16), sb("wds", [INTER, 2, P], F16)

        sg_gate = sb("sg_gate", [P, 4])
        flag = sb("flag", [P, 2])
        memn = sb("memn", [DM, DM + 1])
        bqk_rest = sb("bqk_rest", [P, 8])
        rT = sb("rT", [P, 2, P])
        ffn = sb("ffn", [P, P])

        x2Tn = sb("x2Tn", [P, SEQ])
        x2S = sb("x2S", [P, 2, 2, SEQ], F16)
        cT = sb("cT", [P, 2, NG, SEQ], F16)
        tb = sb("tb", [P, 3, SEQ])
        hh = sb("hh", [P, 3, 2, SEQ], F16)
        ysb = sb("ysb", [P, SEQ])

        stats = [sb(f"stats{n}", [P, NT, 6]) for n in range(4)]
        mv = [sb(f"mv{n}", [P, NT, 2]) for n in range(4)]
        ve = [sb(f"ve{n}", [P, NT]) for n in range(4)]
        rstd = [sb(f"rstd{n}", [P, NT]) for n in range(4)]
        xh01, xh23 = sb("xh01", [P, NT, P]), sb("xh23", [P, NT, P])
        xh = [xh01, xh01, xh23, xh23]

        xin = sb("xin", [P, NT, P])
        x1 = sb("x1", [P, 2, NT, P])
        xT = sb("xT", [P, SEQ])
        x1T = x3T = xT
        low, sg = sb("low", [DM, 2, SEQ]), sb("sg", [DM, 2, SEQ])
        elu = low
        va0 = sb("va0", [P, NT, DM + 1])
        at_cols = [0, SEQ, SEQ + 3 * P, SEQ + 5 * P, SEQ + 6 * P]
        qk = sb("qk", [P, 8, SEQ], F16)
        qt = sb("qt", [P, 2, SEQ], F16)
        AT = qk[:, :, :].rearrange("p a b -> p (a b)").bitcast(F32)
        dn, rc = sb("dn", [P, 8]), sb("rc", [P, 8])
        cmA, cmB, comb = sb("cmA", [P, NT, DM]), sb("cmB", [P, NT, DM]), sb("comb", [P, NT, DM])
        cbT = sb("cbT", [DM, SEQ])
        lg, key, rep, ex = (sb(n, [P, NT, NE]) for n in ("lg", "key", "rep", "ex"))
        sel = rep
        ex1 = prob = wt = cw = ex
        top = sb("top", [P, NT, 8])
        tot = sb("tot", [P, 4, NT])
        parts = sb("parts", [P, NT, NG, 2, GE], F16)

        def grouped(v):
            return v[:, :, :].rearrange("p t (g e) -> p t g e", g=NG)

        rows = sb("rows", [P, 4, NT, P])
        x2, x2b, x3, x3b = (rows[:, k] for k in range(4))
        stage = rows[:, :, :, :].rearrange("p (s a) t e -> p s (a t e)", s=2)
        vf = lg[:, :, :].rearrange("p t e -> p (t e)")[:, 0:(NT + 1) * P].rearrange("p (m e) -> p m e", e=P)
        va = sb("va", [P, NT + 1, NH, 2, HD + 1], F16)
        bvs = sb("bvs", [P, P])
        vs = sb("vs", [P, NH, HD + 1])
        sm = sb("sm", [P, 3, 2, WIN])
        pr = sm
        mn = sb("mn", [P, 3, 2])
        pT = sb("pT", [P, 2, 4, P])
        pS = sb("pS", [P, 2, 2, 4, P], F16)
        rd = sb("rd", [P, NH])
        cx = sb("cx", [P, NT, P])
        cxT = sb("cxT", [P, SEQ])
        x4T = cxT
        osb = sb("osb", [P, NT, P])

        s_a, s_b, s_c, s_x, s_out = sem("s_a"), sem("s_b"), sem("s_c"), sem("s_x"), sem("s_out")
        s_d = sem("s_d")
        s_w = [sem(f"s_w{k}") for k in range(2)]
        s_wr, s_wl = sem("s_wr"), sem("s_wl")
        s_gate, s_memn, s_rT, s_wds = sem("s_gate"), sem("s_memn"), sem("s_rT"), sem("s_wds")
        s_f1, s_f2, s_ffnw, s_ones = sem("s_f1"), sem("s_f2"), sem("s_ffnw"), sem("s_ones")
        s_z, s_t, s_u, s_g, s_h, s_y = (sem(n) for n in ("s_z", "s_t", "s_u", "s_g", "s_h", "s_y"))
        s_hr, s_hl = sem("s_hr"), sem("s_hl")
        s_x2r, s_x2S = sem("s_x2r"), sem("s_x2S")
        f_qk, s_qt, s_qk = sem("f_qk"), sem("s_qt"), sem("s_qk")
        s_wgr = sem("s_wgr")
        s_cw, s_p0 = sem("s_cw"), sem("s_p0")
        s_ysb = sem("s_ysb")
        s_var = [sem(f"s_var{n}") for n in range(4)]
        s_rstd = [sem(f"s_rstd{n}") for n in range(4)]
        s_xh = [sem(f"s_xh{n}") for n in range(4)]
        (f_T1, f_qk0, f_v0, f_num, f_Tcomb, f_oproj, f_T2, f_router, f_cT) = (
            sem(n) for n in ("f_T1", "f_qk0", "f_v0", "f_num", "f_Tcomb", "f_oproj", "f_T2", "f_router", "f_cT"))
        (f_Ty, f_T3, f_v, f_v4, f_Tctx, f_proj, f_T4, f_ffn) = (
            sem(n) for n in ("f_Ty", "f_T3", "f_v", "f_v4", "f_Tctx", "f_proj", "f_T4", "f_ffn"))
        (s_x1T, s_low, s_elu, s_sg, s_v0, s_comb, s_cbT, s_x1, s_x2T, s_lg, s_ex, s_prob, s_wt, s_sc,
         s_parts) = (sem(n) for n in (
             "s_x1T", "s_low", "s_elu", "s_sg", "s_v0", "s_comb", "s_cbT", "s_x1", "s_x2T", "s_lg", "s_ex",
             "s_prob", "s_wt", "s_sc", "s_parts"))
        (s_x2, s_x2b, s_x3T, s_v, s_v4, s_cxT, s_x3, s_x3b, s_x4T, s_o) = (sem(n) for n in (
            "s_x2", "s_x2b", "s_x3T", "s_v", "s_v4", "s_cxT", "s_x3", "s_x3b", "s_x4T", "s_o"))
        f_AT, s_ATd, s_ATc, s_cT = sem("f_AT"), sem("s_ATd"), sem("s_ATc"), sem("s_cT")
        f_sc, s_sm, s_pr, f_pT, s_pT = sem("f_sc"), sem("s_sm"), sem("s_pr"), sem("f_pT"), sem("s_pT")
        s_pr2, s_pl = sem("s_pr2"), sem("s_pl")
        s_vr, s_vl, s_vs = sem("s_vr"), sem("s_vl"), sem("s_vs")
        f_pv, s_cx = sem("f_pv"), sem("s_cx")

        pd = qk[:, :, :].rearrange("p a b -> p (a b)").bitcast(F32)[:, 0:WIDTH_D]
        d = {n: pd[:, lo:hi] for n, (lo, hi) in COL_D.items()}

        xv = x.rearrange("b (t p) h -> b p t h", p=P)
        ov = out.rearrange("b (t p) h -> b p t h", p=P)

        def heads_of(v):
            return v[:, :, :].rearrange("p m (h e) -> p m h e", h=NH)

        block = ctx.enter_context(nc.Block())

        @block.sync
        def _(sp):
            def load_x(b):
                sp.wait_ge(s_x1, b)
                sp.dma_start(xin[:, :, :], xv[b]).then_inc(s_x, 16)

            load_x(0)
            sp.dma_start(pa[:, :], pack_a).then_inc(s_a, 16)
            sp.dma_start(pc[:, :], pack_c).then_inc(s_c, 16)
            sp.dma_start(pd, pack_d).then_inc(s_d, 16)
            sp.dma_start(pb[:, :], pack_b).then_inc(s_b, 16)
            for n in range(2 * NCH):
                k, src = n // 2, (w_up, w_down)[n % 2]
                if n >= 2:
                    sp.wait_ge(s_wl, n - 1)
                sp.dma_start(stage[:, n % 2, :], src[:, k * CH * P:(k + 1) * CH * P]).then_inc(s_w[n % 2], 16)

            def iteration(i, par, before, after):
                if after:
                    load_x(i + 1)
                if before:
                    sp.wait_ge(s_o, i)
                    sp.dma_start(ov[i - 1], osb[:, :, :]).then_inc(s_out, 16)

            def epilogue():
                sp.wait_ge(s_o, NB)
                sp.dma_start(ov[NB - 1], osb[:, :, :]).then_inc(s_out, 16)
                sp.wait_ge(s_out, 16 * NB)

            run_batches(sp, lambda: None, iteration, epilogue)

        @block.tensor
        def _(pe):
            def transposes(bank, src):
                for t in range(NT):
                    last = pe.transpose(side[:, bank, t * P:(t + 1) * P], src(t), a["ident"])
                return last

            def setup():
                pe.wait_ge(s_d, 16)
                for k, (p1, p2, s2) in enumerate((("fr", "fi", "sin"), ("fi", "fr", "nsin"))):
                    pe.matmul(side[:, 1 + k, 0:P], d[p1], d["cos"], start=True, stop=False)
                    last = pe.matmul(side[:, 1 + k, 0:P], d[p2], d[s2], start=False, stop=True)
                last.then_inc(s_f1, 1)
                pe.wait_ge(s_rT, 1)
                pe.matmul(side[:, 1, 0:P], rT[:, 0, :], d["cos"], start=True, stop=False)
                pe.matmul(side[:, 1, 0:P], rT[:, 1, :], d["nsin"], start=False, stop=True).then_inc(s_f2, 1)
                pe.wait_ge(s_ffnw, 1)

            def l0_T1(b, before):
                pe.wait_ge(s_xh[0], b + 1)
                pe.wait_ge(s_cT, NG // 2 * b)
                if before:
                    pe.wait_ge(s_cx, NT * (b - 1))
                transposes(2, lambda t: xh[0][:, t, :]).then_inc(f_T1, 1)

            def l0_qkv(b, before):
                pe.wait_ge(s_x1T, b + 1)
                if before:
                    pe.wait_ge(s_x4T, b - 1)
                    pe.wait_ge(s_o, b - 1)
                pe.matmul(side[0:DM, 0, :], a["wq0"], x1T[:, :], start=True, stop=True)
                pe.matmul(side[0:DM, 1, :], a["wk0"], x1T[:, :], start=True, stop=True).then_inc(f_qk0, 1)
                for t in range(NT):
                    last = pe.matmul(side[:, 2, t * DM:(t + 1) * DM], x1T[:, t * P:(t + 1) * P], a["wv0"],
                                     start=True, stop=True)
                last.then_inc(f_v0, 1)

            def l0_causal(b):
                pe.wait_ge(s_sg, b + 1)
                pe.wait_ge(s_v0, b + 1)
                for bank, kts in enumerate(((0,), (1,), (2, 3))):
                    for kt in kts:
                        at = at_cols[kt] - at_cols[kts[0]]
                        n = SEQ - kt * P
                        last = pe.matmul(side[:, bank, at:at + n], sg[:, 1, kt * P:(kt + 1) * P], sg[:, 0, kt * P:],
                                         start=True, stop=True)
                    last.then_inc(f_AT, 1)

            def l0_num(b):
                pe.wait_ge(s_ATc, 3 * b + 3)
                pe.wait_ge(s_ATd, 4 * b + 4)
                w = DM + 1
                for qt in range(NT):
                    for kt in range(qt + 1):
                        at = at_cols[kt] + (qt - kt) * P
                        pe.matmul(side[:, 0, qt * w:(qt + 1) * w], AT[:, at:at + P], va0[:, kt, :],
                                  start=(kt == 0), stop=(kt == qt))
                for qt in range(NT):
                    last = pe.matmul(side[:, 0, (NT + qt) * w:(NT + qt + 1) * w], sg[:, 0, qt * P:(qt + 1) * P],
                                     memn[:, :], start=True, stop=True)
                last.then_inc(f_num, 1)

            def l0_Tcomb(b):
                pe.wait_ge(s_comb, b + 1)
                for t in range(NT):
                    last = pe.transpose(side[0:DM, 1, t * P:(t + 1) * P], comb[:, t, :], a["ident"])
                last.then_inc(f_Tcomb, 1)

            def l0_oproj(b):
                pe.wait_ge(s_cbT, b + 1)
                for t in range(NT):
                    last = pe.matmul(side[:, 2, t * P:(t + 1) * P], cbT[:, t * P:(t + 1) * P], a["wo0"][0:DM],
                                     start=True, stop=True)
                last.then_inc(f_oproj, 1)

            def l0_T2(b):
                pe.wait_ge(s_xh[1], b + 1)
                transposes(0, lambda t: xh[1][:, t, :]).then_inc(f_T2, 1)

            def l0_router(b):
                pe.wait_ge(s_x2T, b + 1)
                for t in range(NT):
                    last = pe.matmul(side[:, 1 + t // 2, (t % 2) * NE:(t % 2 + 1) * NE], x2Tn[:, t * P:(t + 1) * P],
                                     a["router"], start=True, stop=True)
                last.then_inc(f_router, 1)

            def l0_cT(b):
                pe.wait_ge(s_parts, b + 1)
                pe.wait_ge(s_lg, b + 1)
                for g in range(NG):
                    bank = side[:, g // 2, :].bitcast(F16)
                    for t in range(NT):
                        at = (g % 2) * SEQ + t * P
                        last = pe.transpose(bank[0:2 * GE, at:at + P],
                                            parts[:, t, g, :, :].rearrange("p k e -> p (k e)"), identh)
                    if g % 2:
                        last.then_inc(f_cT, 1)

            def l1_Ty(b, gates):
                pe.wait_ge(s_ysb, b + 1)
                pe.wait_ge(s_cT, NG // 2 * gates)
                if isinstance(b, int) and b == NB - 1:
                    pe.wait_ge(s_o, b)
                transposes(0, lambda t: ysb[:, t * P:(t + 1) * P]).then_inc(f_Ty, 1)

            def l1_T3(b):
                pe.wait_ge(s_xh[2], b + 1)
                transposes(1, lambda t: xh[2][:, t, :]).then_inc(f_T3, 1)

            def l1_qk(b, n):
                if n == 0:
                    pe.wait_ge(s_x3T, b + 1)
                for m, bank in ((2 * n, 0), (2 * n + 1, 2)):
                    if n > 0:
                        pe.wait_ge(s_qk, 8 * b + m - 1)
                    pe.matmul(side[:, bank, :], c["wqk"][:, m * P:(m + 1) * P], x3T[:, :],
                              start=True, stop=True).then_inc(f_qk, 1)

            def l1_v(b):
                for m in range(NT):
                    lo, hi = chunk_tokens(m)
                    last = pe.matmul(side[0:hi - lo, 1, m * P:(m + 1) * P], x3T[:, lo:hi], c["wv"],
                                     start=True, stop=True)
                last.then_inc(f_v, 1)

            def l1_v4(b):
                pe.wait_ge(s_v, b + 1)
                lo, hi = chunk_tokens(NT)
                pe.matmul(side[0:hi - lo, 1, 0:P], x3T[:, lo:hi], c["wv"], start=True, stop=True).then_inc(f_v4, 1)

            def scores(b, w):
                t = w // (NH // 2)
                lo, hi, off = window(t)
                if w == 0:
                    pe.wait_ge(s_qk, 8 * b + 8)
                else:
                    pe.wait_ge(s_sm, NU * b + w)
                for k, (_, g, r) in enumerate(heads(w)):
                    last = pe.matmul(side[:, 0, k * WIN + off:k * WIN + off + hi - lo],
                                     qk[32 * r:32 * r + 32, g, t * P:(t + 1) * P], qk[32 * r:32 * r + 32, 4 + g, lo:hi],
                                     start=True, stop=True)
                last.then_inc(f_sc, 1)

            def turn_probs(b, w):
                t = w // (NH // 2)
                pe.wait_ge(s_pr, NU * b + w + 1)
                if w == 0:
                    pe.wait_ge(s_v4, b + 1)
                else:
                    pe.wait_ge(s_pT, NU * b + w)
                for k in range(2):
                    for cc in ((1, 0) if t == 0 else (0, 1)):
                        col, rows = chunk(t, cc)
                        last = pe.transpose(side[0:rows, 1, (2 * k + cc) * P:(2 * k + cc + 1) * P],
                                            pr[:, w % 3, k, col:col + rows], a["ident"])
                last.then_inc(f_pT, 1)

            def context(b, w):
                t, hp = w // (NH // 2), w % (NH // 2)
                pe.wait_ge(s_pl, NU * b + w + 1)
                if w == 0:
                    pe.wait_ge(s_vl, b + 1)
                if hp == 0 and t > 0:
                    pe.wait_ge(s_cx, NT * b + t)
                for k, (h, _, _) in enumerate(heads(w)):
                    for cc in range(2):
                        _, rows = chunk(t, cc)
                        for part in range(2):
                            last = pe.matmul(side[:, 2, h * VW:(h + 1) * VW], pS[0:rows, w % 2, part, 2 * k + cc, :],
                                             va[0:rows, t + cc, h, :, :].rearrange("p k e -> p (k e)"),
                                             start=(cc == 0 and part == 0), stop=(cc == 1 and part == 1))
                last.then_inc(f_pv, 1)

            def l1_Tctx(b):
                pe.wait_ge(s_cx, NT * b + NT)
                pe.wait_ge(s_sm, NU * b + NU)
                transposes(0, lambda t: cx[:, t, :]).then_inc(f_Tctx, 1)

            def project(f_sem, srcT, w):
                for t in range(NT):
                    last = pe.matmul(side[:, 1, t * P:(t + 1) * P], srcT[:, t * P:(t + 1) * P], w, start=True, stop=True)
                last.then_inc(f_sem, 1)

            def l1_proj(b):
                pe.wait_ge(s_cxT, b + 1)
                pe.wait_ge(s_pT, NU * b + NU)
                project(f_proj, cxT, c["wo"])

            def l1_T4(b):
                pe.wait_ge(s_xh[3], b + 1)
                transposes(0, lambda t: xh[3][:, t, :]).then_inc(f_T4, 1)

            def l1_ffn(b):
                pe.wait_ge(s_x4T, b + 1)
                pe.wait_ge(s_x3, b + 1)
                project(f_ffn, x4T, ffn[:, :])

            def three_passes(acc, w, v, start, stop):
                pe.matmul(acc, w(0), v(0), start=start, stop=False)
                pe.matmul(acc, w(0), v(1), start=False, stop=False)
                return pe.matmul(acc, w(1), v(0), start=False, stop=stop)

            def up(i, par, j, before):
                if j == 0:
                    pe.wait_ge(s_x2S, i + 1)
                if before or j >= 2:
                    pe.wait_ge(s_u, NJ * i + j - 1)
                n, w = (P, lambda k: wup[:, k, j, :]) if j < NP else (INTER, lambda k: wgs[:, k, :])
                three_passes(zp[0:n, (par + j) % 2, :], w, lambda k: x2S[:, par, k, :], True, True).then_inc(s_z, 1)

            def gates(i, par, j, before):
                if j == 0:
                    pe.wait_ge(s_cT, NG // 2 * (i + 1))
                if before or j >= 2:
                    pe.wait_ge(s_h, NJ * i + j - (1 if j >= 2 else 2))
                g, u = j // PPG, j % PPG
                pe.matmul(gp[:, j % 2, :], spread[0:2 * GE, u * P:(u + 1) * P], cT[0:2 * GE, par, g, :],
                          start=True, stop=True).then_inc(s_g, 1)

            def down(i, j):
                if j == 0:
                    pe.wait_ge(s_ysb, i)
                pe.wait_ge(s_hl, NJ * i + j + 1)
                n, w = (P, lambda k: wdn[:, k, j, :]) if j < NP else (INTER, lambda k: wds[:, k, :])
                three_passes(yp[:, :], w, lambda k: hh[0:n, j % 3, k, :], j == 0, j == NP).then_inc(s_y, 1)

            def banded(b, s, g):
                w = s - UNITS
                if s == Y_BACK:
                    l1_Ty(b, g)
                if s == T3:
                    l1_T3(b)
                if QKV <= s < QKV + 4:
                    l1_qk(b, s - QKV)
                if s == QKV:
                    l1_v(b)
                if s == QKV + 3:
                    l1_v4(b)
                if 0 <= w - 3 < NU:
                    turn_probs(b, w - 3)
                if s == POST:
                    l1_Tctx(b)
                if s == PROJ:
                    l1_proj(b)
                if s == T4:
                    l1_T4(b)
                if s == FFN:
                    l1_ffn(b)

            def late(b, s):
                if 0 <= s - UNITS - 5 < NU:
                    context(b, s - UNITS - 5)
                if 0 <= s - UNITS < NU:
                    scores(b, s - UNITS)

            def linear(b, s, before):
                if s == T1:
                    l0_T1(b, before)
                if s == QKV0:
                    l0_qkv(b, before)
                if s == CAUSAL:
                    l0_causal(b)
                if s == NUM:
                    l0_num(b)
                if s == TCOMB:
                    l0_Tcomb(b)
                if s == OPROJ:
                    l0_oproj(b)
                if s == T2:
                    l0_T2(b)
                if s == ROUTER:
                    l0_router(b)
                if s == CT:
                    l0_cT(b)

            def iteration(i, par, before, after):
                for s in range(NJ):
                    if not before and s % CH == 0 and s < NP:
                        pe.wait_ge(s_wl, 2 * (s // CH) + 2)
                    up(i, par, s, before)
                    if s < NP:
                        gates(i, par, s, before)
                    if before:
                        banded(i - 1, s, i + 1)
                    if after:
                        linear(i + 1, s, before)
                    if s >= 3:
                        down(i, s - 3)
                    elif before:
                        down(i - 1, NJ - 3 + s)
                    if before:
                        late(i - 1, s)

            def prologue():
                pe.wait_ge(s_a, 16)
                pe.wait_ge(s_c, 16)
                setup()
                pe.wait_ge(s_memn, 1)
                pe.wait_ge(s_ones, 2)
                for s in range(NJ):
                    linear(0, s, False)
                pe.wait_ge(s_wds, 1)

            def epilogue():
                for j in range(NJ - 3, NJ):
                    down(NB - 1, j)
                for s in range(NJ):
                    banded(NB - 1, s, NB)
                    late(NB - 1, s)

            run_batches(pe, prologue, iteration, epilogue)

        @block.scalar
        def _(act):
            def setup():
                act.wait_ge(s_a, 16)
                act.activation(sg_gate[:, 0:1], a["gate"], ACT.Exp, scale=-1.0).then_inc(s_gate, 1)
                act.wait_ge(s_f1, 1)
                act.activation(rT[:, :, :], side[:, 1:3, 0:P], ACT.Copy).then_inc(s_rT, 1)
                act.wait_ge(s_f2, 1)
                act.activation(ffn[:, :], side[:, 1, 0:P], ACT.Copy, scale=1.0 / H).then_inc(s_ffnw, 1)

            def out_of_psum(dst, bank, full, value, done):
                act.wait_ge(full, value)
                act.activation(dst, side[:, bank, :], ACT.Copy).then_inc(done, 1)

            def linear(b, par, s):
                if s == T1:
                    out_of_psum(x1T[:, :], 2, f_T1, b + 1, s_x1T)
                if s == QKV0:
                    act.wait_ge(f_v0, b + 1)
                    act.activation(va0[:, :, 0:DM], side[:, 2, 0:NT * DM].rearrange("p (t e) -> p t e", t=NT),
                                   ACT.Copy).then_inc(s_v0, 1)
                if s == QKV0 + 1:
                    act.wait_ge(s_low, b + 1)
                    act.activation(elu[:, :, :], low[:, :, :], ACT.Exp).then_inc(s_elu, 1)
                if s == CAUSAL + 1:
                    for bank, kt in enumerate((0, 1, 2)):
                        act.wait_ge(s_ATd, 4 * b + (1, 2, 4)[bank])
                        act.activation(AT[:, at_cols[kt] + P:at_cols[kt + 1]],
                                       side[:, bank, P:SEQ - kt * P], ACT.Copy).then_inc(s_ATc, 1)
                if s == TCOMB:
                    act.wait_ge(f_Tcomb, b + 1)
                    act.activation(cbT[:, :], side[0:DM, 1, :], ACT.Copy).then_inc(s_cbT, 1)
                if s == T2:
                    out_of_psum(x2Tn[:, :], 0, f_T2, b + 1, s_x2T)
                    act.wait_ge(s_x2T, b + 1)
                    act.activation(x2S[:, par, 0, :], x2Tn[:, :], ACT.Copy).then_inc(s_x2r, 1)
                if s == ROUTER + 1:
                    act.wait_ge(s_lg, b + 1)
                    act.activation(ex[:, :, :], lg[:, :, :], ACT.Exp, scale=-1.0).then_inc(s_ex, 1)
                if s == GATES + 1:
                    act.wait_ge(s_cw, b + 1)
                    act.activation(parts[:, :, :, 0, :], grouped(cw), ACT.Copy).then_inc(s_p0, 1)
                if s == CT:
                    for k in range(NG // 2):
                        act.wait_ge(f_cT, NG // 2 * b + k + 1)
                        act.activation(cT[0:2 * GE, par, 2 * k:2 * k + 2, :].rearrange("p g t -> p (g t)"),
                                       side[0:2 * GE, k, :].bitcast(F16), ACT.Copy).then_inc(s_cT, 1)

            def banded(b, s):
                w = s - UNITS
                if s == T3:
                    out_of_psum(x3T[:, :], 1, f_T3, b + 1, s_x3T)
                if QKV <= s < QKV + 4:
                    for m, bank in ((2 * (s - QKV), 0), (2 * (s - QKV) + 1, 2)):
                        act.wait_ge(f_qk, 8 * b + m + 1)
                        act.wait_ge(s_qk, 8 * b + m - 1) if m >= 2 else None
                        act.activation(qt[:, m % 2, :], side[:, bank, :], ACT.Identity, scale=c["rest"][:, m // 4:m // 4 + 1],
                                       bias=bqk_rest[:, m:m + 1]).then_inc(s_qt, 1)
                if 0 <= w - 3 < NU:
                    probs(b, w - 3)
                if 0 <= w - 1 < NU:
                    exps(b, w - 1)
                if s == POST:
                    out_of_psum(cxT[:, :], 0, f_Tctx, b + 1, s_cxT)
                if s == T4:
                    out_of_psum(x4T[:, :], 0, f_T4, b + 1, s_x4T)

            def exps(b, w):
                lo, hi, off = window(w // (NH // 2))
                act.wait_ge(s_sm, NU * b + w + 1)
                for k in range(2):
                    last = act.activation(pr[:, w % 3, k, off:off + hi - lo], sm[:, w % 3, k, off:off + hi - lo],
                                          ACT.Exp, scale=-1.0, bias=mn[:, w % 3, k:k + 1])
                last.then_inc(s_pr, 1)

            def probs(b, w):
                t = w // (NH // 2)
                act.wait_ge(f_pT, NU * b + w + 1)
                src = side[:, 1, :].rearrange("p (k q) -> p k q", k=4)
                if w >= 2:
                    act.wait_ge(s_pl, NU * b + w - 1)
                if 0 < t < NT - 1:
                    act.activation(pT[:, w % 2, :, :], src, ACT.Copy, scale=PS).then_inc(s_pT, 1)
                    return
                for cc in range(2):
                    _, rows = chunk(t, cc)
                    last = act.activation(pT[0:rows, w % 2, cc::2, :], src[0:rows, cc::2, :], ACT.Copy, scale=PS)
                last.then_inc(s_pT, 1)

            def rounded(i, j):
                n = P if j < NP else INTER
                act.wait_ge(s_h, NJ * i + j + 1)
                if j >= 3 or not (isinstance(i, int) and i == 0):
                    act.wait_ge(s_y, NJ * i + j - 2)
                act.activation(hh[0:n, j % 3, 0, :], tb[0:n, j % 3, :], ACT.Copy).then_inc(s_hr, 1)

            def iteration(i, par, before, after):
                for s in range(NJ):
                    if s == 3 and before:
                        act.wait_ge(s_y, NJ * i)
                        act.activation(ysb[:, :], yp[:, :], ACT.Copy, scale=1.0 / WS).then_inc(s_ysb, 1)
                    if before and s > 0:
                        banded(i - 1, s - 1)
                    if after and s > 0:
                        linear(i + 1, 1 - par, s - 1)
                    n = P if s < NP else INTER
                    act.wait_ge(s_z, NJ * i + s + 1)
                    if before or s >= 3:
                        act.wait_ge(s_hl, NJ * i + s - 2)
                    act.activation(tb[0:n, s % 3, :], zp[0:n, (par + s) % 2, :], ACT.Tanh,
                                   scale=0.5 / WS).then_inc(s_t, 1)
                    if s >= 1:
                        rounded(i, s - 1)
                    elif before:
                        rounded(i - 1, NJ - 1)

            def round_weights():
                for n in range(2 * NCH):
                    k, dst = n // 2, (wup, wdn)[n % 2]
                    act.wait_ge(s_w[n % 2], 16 * (n // 2 + 1))
                    act.activation(dst[:, 0, k * CH:(k + 1) * CH, :], stage[:, n % 2, :].rearrange(
                        "p (j e) -> p j e", j=CH), ACT.Copy, scale=WS).then_inc(s_wr, 1)

            def prologue():
                setup()
                act.wait_ge(s_b, 16)
                act.activation(wgs[:, 0, :], c["wgs"], ACT.Copy, scale=WS)
                act.activation(wds[:, 0, :], c["wds"][0:INTER], ACT.Copy, scale=WS).then_inc(s_wgr, 1)
                for s in range(NJ):
                    linear(0, 0, s)
                round_weights()

            def epilogue():
                rounded(NB - 1, NJ - 1)
                act.wait_ge(s_y, NJ * NB)
                act.activation(ysb[:, :], yp[:, :], ACT.Copy, scale=1.0 / WS).then_inc(s_ysb, 1)
                for s in range(NJ):
                    banded(NB - 1, s)

            run_batches(act, prologue, iteration, epilogue)

        @block.vector
        def _(dve):
            def link(ins, wait=True):
                if wait:
                    dve.drain()

            def setup():
                dve.memset(va0[:, :, DM:DM + 1], 1.0).then_inc(s_ones, 1)
                dve.memset(pT[:, :, :, :], 0.0)
                dve.memset(va[:, :, :, 0, HD:HD + 1], WS)
                dve.memset(va[:, :, :, 1, HD:HD + 1], 0.0).then_inc(s_ones, 1)
                dve.wait_ge(s_a, 16)
                dve.wait_ge(s_gate, 1)
                link(dve.tensor_scalar(sg_gate[:, 1:2], sg_gate[:, 0:1], 1.0, None, ALU.add))
                link(dve.reciprocal(sg_gate[:, 2:3], sg_gate[:, 1:2]))
                link(dve.tensor_scalar(sg_gate[:, 3:4], sg_gate[:, 2:3], -1.0, 1.0, ALU.mult, ALU.add))
                link(dve.tensor_reduce(flag[:, 0:1], a["normrow"], AX.X, ALU.add))
                link(dve.tensor_scalar(flag[:, 1:2], flag[:, 0:1], EPS, None, ALU.is_ge))
                link(dve.tensor_scalar(memn[:, 0:DM], a["mem"][0:DM], sg_gate[0:DM, 2:3], flag[0:DM, 1:2],
                                       ALU.mult, ALU.mult))
                dve.tensor_copy(memn[:, DM:DM + 1], a["norm"][0:DM]).then_inc(s_memn, 1)

            def rest(dst, src):
                return dve.scalar_tensor_tensor(dst(1), src, WS, dst(0), ALU.mult, ALU.subtract)

            def late_setup():
                dve.wait_ge(s_b, 16)
                dve.tensor_scalar(bvs[:, :], c["bv"], WS, None, ALU.mult)
                for k in range(2):
                    last = dve.tensor_scalar(bqk_rest[:, 4 * k:4 * k + 4], c["bqk"][:, 4 * k:4 * k + 4],
                                             c["rest"][:, k:k + 1], None, ALU.mult)
                dve.wait_ge(s_wgr, 1)
                rest(lambda k: wgs[:, k, :], c["wgs"])
                rest(lambda k: wds[:, k, :], c["wds"][0:INTER]).then_inc(s_wds, 1)
                for n in range(2 * NCH):
                    k, dst = n // 2, (wup, wdn)[n % 2]
                    dve.wait_ge(s_wr, n + 1)
                    rest(lambda q: dst[:, q, k * CH:(k + 1) * CH, :],
                         stage[:, n % 2, :].rearrange("p (j e) -> p j e", j=CH)).then_inc(s_wl, 1)

            def norm_stats(n, src, b):
                for t in range(NT):
                    link(dve.bn_stats(stats[n][:, t, :], src[:, t, :]), wait=(t == NT - 1))
                for t in range(NT):
                    last = dve.bn_aggr(mv[n][:, t, :], stats[n][:, t, :])
                last.then_inc(s_var[n], 1)

            def norm_apply(n, src, b):
                dve.wait_ge(s_rstd[n], b + 1)
                for t in range(NT):
                    last = dve.tensor_scalar(xh[n][:, t, :], src[:, t, :], mv[n][:, t, 0:1], rstd[n][:, t:t + 1],
                                             ALU.subtract, ALU.mult)
                last.then_inc(s_xh[n], 1)

            def tiles(ap):
                return ap.rearrange("p (t e) -> p t e", t=NT)

            def linear(b, par, s):
                if s == LN1_A:
                    dve.wait_ge(s_x, 16 * b + 16)
                    norm_stats(0, xin, b)
                if s == LN1_B:
                    norm_apply(0, xin, b)
                if s == QKV0:
                    dve.wait_ge(f_qk0, b + 1)
                    dve.tensor_scalar(low[:, :, :], side[0:DM, 0:2, :], 0.0, None, ALU.min).then_inc(s_low, 1)
                if s == QKV0 + 2:
                    dve.wait_ge(s_elu, b + 1)
                    dve.scalar_tensor_tensor(sg[:, :, :], side[0:DM, 0:2, :], 0.0, elu[:, :, :], ALU.max,
                                             ALU.add).then_inc(s_sg, 1)
                if s == CAUSAL:
                    for bank, kt in ((0, 0), (1, 1), (2, 2), (2, 3)):
                        dve.wait_ge(f_AT, 3 * b + bank + 1)
                        at = 2 * P if kt == 3 else 0
                        dve.tensor_tensor(AT[:, at_cols[kt]:at_cols[kt] + P], side[:, bank, at:at + P], a["causal"],
                                          ALU.mult).then_inc(s_ATd, 1)
                if s == NUM:
                    dve.wait_ge(f_num, b + 1)
                    v = side[:, 0, 0:8 * (DM + 1)].rearrange("p (m e) -> p m e", m=8)
                    link(dve.tensor_scalar(dn[:, :].unsqueeze(2), v[:, :, DM:DM + 1], EPS, None, ALU.max))
                    link(dve.reciprocal(rc[:, :], dn[:, :]))
                    link(dve.tensor_scalar(rc[:, 0:NT], rc[:, 0:NT], sg_gate[:, 3:4], None, ALU.mult))
                    for dst, lo in ((cmA, 0), (cmB, NT)):
                        link(dve.tensor_tensor(dst[:, :, :], v[:, lo:lo + NT, 0:DM],
                                               rc[:, lo:lo + NT].unsqueeze(2).to_broadcast([P, NT, DM]), ALU.mult),
                             wait=(lo == NT))
                    dve.tensor_tensor(comb[:, :, :], cmA[:, :, :], cmB[:, :, :], ALU.add).then_inc(s_comb, 1)
                if s == OPROJ:
                    dve.wait_ge(f_oproj, b + 1)
                    dve.tensor_tensor(x1[:, par], tiles(side[:, 2, :]), xin[:, :, :], ALU.add).then_inc(s_x1, 1)
                    dve.wait_ge(s_x1, b + 1)
                    norm_stats(1, x1[:, par], b)
                if s == LN2_B:
                    norm_apply(1, x1[:, par], b)
                if s == T2 + 1:
                    dve.wait_ge(s_x2r, b + 1)
                    dve.tensor_tensor(x2S[:, par, 1, :], x2Tn[:, :], x2S[:, par, 0, :], ALU.subtract).then_inc(s_x2S, 1)
                if s == ROUTER:
                    dve.wait_ge(f_router, b + 1)
                    dve.tensor_tensor(lg[:, :, :].rearrange("p (u v) e -> p u (v e)", u=2), side[:, 1:3, 0:2 * NE],
                                      a["ebias"].unsqueeze(1).to_broadcast([P, 2, 2 * NE]), ALU.add).then_inc(s_lg, 1)
                    dve.wait_ge(s_lg, b + 1)
                    link(dve.tensor_scalar(key[:, :, :], lg[:, :, :], SAT, -87.0, ALU.min, ALU.max))
                if s == ROUTER + 1:
                    for t in range(NT):
                        link(dve.max(top[:, t, :], key[:, t, :]), wait=(t == NT - 1))
                if s == ROUTER + 2:
                    for t in range(NT):
                        link(dve.match_replace(rep[:, t, :], top[:, t, :], key[:, t, :], -BIG), wait=(t == NT - 1))
                if s == ROUTER + 3:
                    dve.wait_ge(s_ex, b + 1)
                    dve.tensor_scalar(ex1[:, :, :], ex[:, :, :], 1.0, None, ALU.add)
                    link(dve.tensor_tensor(sel[:, :, :], rep[:, :, :], key[:, :, :], ALU.not_equal))
                    dve.reciprocal(prob[:, :, :], ex1[:, :, :]).then_inc(s_prob, 1)
                if s == GATES:
                    dve.wait_ge(s_wt, b + 1)
                    link(dve.tensor_reduce(tot[:, 0, :], wt[:, :, :], AX.X, ALU.add))
                    link(dve.tensor_scalar(tot[:, 1, :], tot[:, 0, :], GATE_EPS, None, ALU.add))
                    link(dve.reciprocal(tot[:, 2, :], tot[:, 1, :]))
                    link(dve.tensor_scalar(tot[:, 3, :], tot[:, 2, :], GS * ROUTED_SCALE / 2 / WS, None, ALU.mult))
                    dve.tensor_tensor(cw[:, :, :], wt[:, :, :], tot[:, 3, :].unsqueeze(2).to_broadcast([P, NT, NE]),
                                      ALU.mult).then_inc(s_cw, 1)
                if s == GATES + 2:
                    dve.wait_ge(s_p0, b + 1)
                    dve.tensor_tensor(parts[:, :, :, 1, :], grouped(cw), parts[:, :, :, 0, :],
                                      ALU.subtract).then_inc(s_parts, 1)

            def banded(b, par, s):
                w = s - UNITS
                if s == Y_BACK:
                    dve.wait_ge(f_Ty, b + 1)
                    dve.tensor_tensor(x2[:, :, :], tiles(side[:, 0, :]), x1[:, par], ALU.add).then_inc(s_x2, 1)
                    dve.wait_ge(s_x2, b + 1)
                    norm_stats(2, x2, b)
                if s == LN3_B:
                    norm_apply(2, x2, b)
                if QKV <= s < QKV + 4:
                    for m, bank in ((2 * (s - QKV), 0), (2 * (s - QKV) + 1, 2)):
                        dve.wait_ge(s_qt, 8 * b + m + 1)
                        dve.scalar_tensor_tensor(qk[:, m, :], side[:, bank, :], c["bqk"][:, m:m + 1], qt[:, m % 2, :],
                                                 ALU.add, ALU.subtract).then_inc(s_qk, 1)
                if s == QKV + 1:
                    dve.wait_ge(f_v, b + 1)
                    for m in range(NT):
                        last = values(m, 1, m * P)
                    last.then_inc(s_v, 1)
                if s == QKV + 4:
                    dve.wait_ge(f_v4, b + 1)
                    values(NT, 1, 0).then_inc(s_v4, 1)
                    dve.wait_ge(s_v4, b + 1)
                    dve.tensor_copy(va[:, :, :, 0, 0:HD], heads_of(vf)).then_inc(s_vr, 1)
                if 0 <= w - 3 < NU:
                    if w >= 5:
                        dve.wait_ge(f_pv, NU * b + w - 4)
                    dve.wait_ge(s_pT, NU * b + w - 2)
                    dve.tensor_copy(pS[:, (w - 3) % 2, 0], pT[:, (w - 3) % 2]).then_inc(s_pr2, 1)
                if 0 <= w < NU:
                    masked(b, w)
                if w >= 5 and (w - 5) % (NH // 2) == NH // 2 - 1 and w - 5 < NU:
                    t = (w - 5) // (NH // 2)
                    dve.wait_ge(f_pv, NU * b + (t + 1) * NH // 2)
                    v = side[:, 2, 0:NH * VW].rearrange("p (h k e) -> p h e k", h=NH, k=2)
                    dve.tensor_reduce(vs[:, :, :], v, AX.X, ALU.add).then_inc(s_vs, 1)
                    dve.wait_ge(s_vs, NT * b + t + 1)
                    link(dve.reciprocal(rd[:, :].unsqueeze(2), vs[:, :, HD:HD + 1]))
                    dve.tensor_tensor(cx[:, t, :].rearrange("p (h e) -> p h e", h=NH), vs[:, :, 0:HD],
                                      rd[:, :].unsqueeze(2).to_broadcast([P, NH, HD]), ALU.mult).then_inc(s_cx, 1)
                if s == PROJ:
                    dve.wait_ge(f_proj, b + 1)
                    dve.wait_ge(s_x2b, b + 1)
                    dve.tensor_tensor(x3[:, :, :], tiles(side[:, 1, :]), x2b[:, :, :], ALU.add).then_inc(s_x3, 1)
                    dve.wait_ge(s_x3, b + 1)
                    norm_stats(3, x3, b)
                if s == LN4_B:
                    norm_apply(3, x3, b)
                if s == FFN:
                    dve.wait_ge(f_ffn, b + 1)
                    dve.wait_ge(s_x3b, b + 1)
                    dve.tensor_tensor(osb[:, :, :], tiles(side[:, 1, :]), x3b[:, :, :], ALU.add).then_inc(s_o, 1)

            def values(m, bank, at):
                lo, hi = chunk_tokens(m)
                n = hi - lo
                return dve.scalar_tensor_tensor(vf[0:n, m, :], side[0:n, bank, at:at + P], WS, bvs[0:n, :],
                                                ALU.mult, ALU.add)

            def wait_scores(b, w):
                dve.wait_ge(f_sc, NU * b + w + 1)
                if w >= 3:
                    dve.wait_ge(f_pT, NU * b + w - 2)

            def masked(b, w):
                lo, hi, off = window(w // (NH // 2))
                n = hi - lo
                for k in range(2):
                    last = dve.tensor_tensor_reduce(sm[:, w % 3, k, off:off + n],
                                                    side[:, 0, k * WIN + off:k * WIN + off + n],
                                                    c["band"][:, off:off + n], -1.0 / HD ** 0.5, 3e38, ALU.add, ALU.min,
                                                    mn[:, w % 3, k:k + 1])
                last.then_inc(s_sm, 1)

            def gated(i, j):
                dve.wait_ge(s_u, NJ * i + j + 1)
                if j < NP:
                    dve.wait_ge(s_g, NP * i + j + 1)
                    dve.tensor_tensor(tb[:, j % 3, :], gp[:, j % 2, :], tb[:, j % 3, :], ALU.mult).then_inc(s_h, 1)
                else:
                    dve.tensor_scalar(tb[0:INTER, j % 3, :], tb[0:INTER, j % 3, :], 0.5 / WS, None,
                                      ALU.mult).then_inc(s_h, 1)

            def iteration(i, par, before, after):
                for s in range(NJ):
                    if before and 0 <= s - 1 - UNITS < NU:
                        wait_scores(i - 1, s - 1 - UNITS)
                    if s >= 1:
                        gated(i, s - 1)
                    elif before:
                        gated(i - 1, NJ - 1)
                    if before and s > 0:
                        banded(i - 1, 1 - par, s - 1)
                    if after and s > 0:
                        linear(i + 1, 1 - par, s - 1)
                    n = P if s < NP else INTER
                    dve.wait_ge(s_t, NJ * i + s + 1)
                    dve.scalar_tensor_tensor(tb[0:n, s % 3, :], tb[0:n, s % 3, :], 1.0, zp[0:n, (par + s) % 2, :],
                                             ALU.add, ALU.mult).then_inc(s_u, 1)
                if before:
                    dve.wait_ge(s_out, 16 * i)

            def prologue():
                setup()
                for s in range(NJ):
                    linear(0, 0, s)
                late_setup()

            def epilogue():
                gated(NB - 1, NJ - 1)
                for s in range(NJ):
                    if 0 <= s - UNITS < NU:
                        wait_scores(NB - 1, s - UNITS)
                    banded(NB - 1, 1, s)

            run_batches(dve, prologue, iteration, epilogue)

        @block.gpsimd
        def _(pool):
            def rest(i, j):
                n = P if j < NP else INTER
                pool.wait_ge(s_hr, NJ * i + j + 1)
                pool.tensor_tensor(hh[0:n, j % 3, 1, :], tb[0:n, j % 3, :], hh[0:n, j % 3, 0, :],
                                   ALU.subtract).then_inc(s_hl, 1)

            def inverse_root(n, b):
                pool.wait_ge(s_var[n], b + 1)
                pool.tensor_tensor(ve[n][:, :].unsqueeze(2), mv[n][:, :, 1:2], a["eps"].unsqueeze(2), ALU.add)
                pool.drain()
                pool.tensor_tensor(rstd[n][:, :], ve[n][:, :], a["mhalf"], ALU.pow).then_inc(s_rstd[n], 1)

            def linear(b, s):
                if s == LN1_A:
                    inverse_root(0, b)
                if s == OPROJ:
                    inverse_root(1, b)
                if s == GATES - 2:
                    pool.wait_ge(s_prob, b + 1)
                    pool.tensor_tensor(wt[:, :, :], prob[:, :, :], sel[:, :, :], ALU.mult).then_inc(s_wt, 1)

            def banded(b, s):
                bias = lambda n: c[n].unsqueeze(1).to_broadcast([P, NT, P])
                if s == Y_BACK:
                    inverse_root(2, b)
                    pool.tensor_tensor(x2b[:, :, :], x2[:, :, :], bias("bo"), ALU.add).then_inc(s_x2b, 1)
                if s == PROJ:
                    inverse_root(3, b)
                    pool.tensor_tensor(x3b[:, :, :], x3[:, :, :], bias("fbias"), ALU.add).then_inc(s_x3b, 1)
                if s == UNITS + 1:
                    pool.wait_ge(s_vr, b + 1)
                    pool.tensor_tensor(va[:, :, :, 1, 0:HD], heads_of(vf), va[:, :, :, 0, 0:HD],
                                       ALU.subtract).then_inc(s_vl, 1)
                w = s - UNITS - 3
                if 0 <= w < NU:
                    pool.wait_ge(s_pr2, NU * b + w + 1)
                    pool.tensor_tensor(pS[:, w % 2, 1], pT[:, w % 2], pS[:, w % 2, 0], ALU.subtract).then_inc(s_pl, 1)

            def iteration(i, par, before, after):
                for s in range(NJ):
                    if s >= 1:
                        rest(i, s - 1)
                    elif before:
                        rest(i - 1, NJ - 1)
                    if before and s > 0:
                        banded(i - 1, s - 1)
                    if after and s > 0:
                        linear(i + 1, s - 1)

            def prologue():
                pool.wait_ge(s_a, 16)
                for s in range(NJ):
                    linear(0, s)
                pool.wait_ge(s_b, 16)

            def epilogue():
                rest(NB - 1, NJ - 1)
                for s in range(NJ):
                    banded(NB - 1, s)

            run_batches(pool, prologue, iteration, epilogue)


def packed(pack, parts):
    cols, width = columns(pack)
    out = np.zeros((P, width), np.float32)
    for name, (lo, hi) in cols.items():
        out[:parts[name].shape[0], lo:hi] = parts[name]
    return out


def stacked(q, k):
    out = np.zeros((q.shape[0], 2, NH, 32), np.float32)
    for n, v in enumerate((q, k)):
        for copy in range(3):
            out[:, n, :, copy * HD:(copy + 1) * HD] = v.reshape(-1, NH, HD)
    return out.reshape(q.shape[0], 8 * P)


def shape_constants():
    k = np.arange(P)
    angle = 2 * np.pi * ((k[:, None] * k[None, :]) % P) / P
    col = np.arange(WIN)
    part = (k % 32) // HD
    rest = np.stack([part == 2, part == 1], axis=1)
    spread = np.zeros((P, PPG * P), np.float32)
    for row in range(2 * GE):
        for_expert = row % GE
        spread[row, for_expert * INTER:(for_expert + 1) * INTER] = 1.0 / GS
    return {
        "ident": np.eye(P), "causal": (k[None, :] >= k[:, None]).astype(np.float32), "mhalf": np.full((P, NT), -0.5),
        "eps": np.full((P, NT), LN_EPS),
        "band": np.where((col[None, :] >= k[:, None]) & (col[None, :] <= k[:, None] + 2 * HALF), 0.0, -BIG),
        "rest": rest.astype(np.float32),
        "cos": np.cos(angle), "sin": np.sin(angle), "nsin": -np.sin(angle),
    }, spread


def kernel(L0_attn_hidden_states, L0_attn_w_q, L0_attn_w_k, L0_attn_w_v, L0_attn_w_o, L0_attn_gate, L0_attn_memory,
           L0_attn_memory_norm, L0_ffn_router_w, L0_ffn_expert_bias, L0_ffn_w_gate, L0_ffn_w_down,
           L0_ffn_w_gate_shared, L0_ffn_w_down_shared, L1_attn_Wq, L1_attn_bq, L1_attn_Wk, L1_attn_bk, L1_attn_Wv,
           L1_attn_bv, L1_attn_Wo, L1_attn_bo, L1_ffn_w_freq_real, L1_ffn_w_freq_imag, L1_ffn_bias):
    import concourse.bacc as bacc
    from concourse.bass_utils import run_bass_kernel_spmd

    const, spread = shape_constants()
    rows = lambda v, n=P: np.broadcast_to(np.asarray(v)[None, :], (n, np.asarray(v).shape[0]))
    T = lambda v: np.asarray(v).T
    col = lambda v: np.asarray(v)[:, None]
    bias2 = np.concatenate([np.asarray(L0_ffn_expert_bias)] * 2)
    in_a = packed(PACK_A, {
        **const, "wq0": T(L0_attn_w_q), "wk0": T(L0_attn_w_k), "wv0": T(L0_attn_w_v), "router": T(L0_ffn_router_w),
        "ebias": rows(bias2), "gate": rows(L0_attn_gate), "wo0": T(L0_attn_w_o), "mem": np.asarray(L0_attn_memory),
        "norm": col(L0_attn_memory_norm), "normrow": rows(L0_attn_memory_norm)})
    wqk, bqk = stacked(T(L1_attn_Wq), T(L1_attn_Wk)), stacked(rows(L1_attn_bq, 1), rows(L1_attn_bk, 1))
    in_b = packed(PACK_B, {
        **const, "wqk": wqk, "bqk": bqk.reshape(8, P).T, "wv": T(L1_attn_Wv), "wo": T(L1_attn_Wo),
        "bv": rows(L1_attn_bv), "bo": rows(L1_attn_bo), "fbias": rows(L1_ffn_bias),
        "wgs": T(L0_ffn_w_gate_shared), "wds": T(L0_ffn_w_down_shared)})
    in_d = packed(PACK_D, {
        **const, "fr": np.asarray(L1_ffn_w_freq_real), "fi": np.asarray(L1_ffn_w_freq_imag)})
    in_c = np.concatenate([spread, np.eye(P, dtype=np.float32)], axis=1).astype(np.float16)
    up = np.ascontiguousarray(np.asarray(L0_ffn_w_gate).transpose(2, 0, 1).reshape(H, NE * INTER))
    down = np.ascontiguousarray(
        np.asarray(L0_ffn_w_down).reshape(NP, 2, H, INTER).transpose(1, 3, 0, 2).reshape(P, NP * H))

    nc = bacc.Bacc("TRN2", target_bir_lowering=False, num_devices=1)
    arrays = {"in_x": np.ascontiguousarray(L0_attn_hidden_states), "in_a": in_a, "in_b": in_b, "in_c": in_c, "in_d": in_d,
              "in_up": up, "in_down": down}
    aps = [nc.dram_tensor(n, v.shape, mybir.dt.from_np(v.dtype), kind="ExternalInput").ap() for n, v in arrays.items()]
    out = nc.dram_tensor("out_y", (NB, SEQ, H), F32, kind="ExternalOutput").ap()
    build(nc, *aps, out)
    r = run_bass_kernel_spmd(nc, [arrays], core_ids=[0])
    return r.results[0]["out_y"]
```

```python
from contextlib import ExitStack

import numpy as np

import concourse.bass as bass
from concourse import mybir

F32 = mybir.dt.float32
F16 = mybir.dt.float16
ALU = mybir.AluOpType
ACT = mybir.ActivationFunctionType
AX = mybir.AxisListType

NB, SEQ, H = 8, 512, 128
P = 128
NT = SEQ // P
DM = 32
NE, INTER = 160, 64
NP = NE // 2
NJ = NP + 1
GE = 40
NG = NE // GE
PPG = GE // 2
NH, HD = 16, 8
HALF = 64
WIN = P + 2 * HALF
PS = 2.0 ** 15
VW = 2 * (HD + 1)
NU = NT * NH // 2
LN_EPS, EPS, GATE_EPS = 1e-5, 1e-6, 1e-9
ROUTED_SCALE = 2.5
SAT = 16.64
BIG = 1e30
WS = 16.0
GS = 1024.0
CH = 8
NCH = NP // CH

PACK_A = [("ident", P), ("wqk0", 2 * DM), ("wv0", DM), ("causal", P), ("router", NE), ("ebias", 2 * NE),
          ("gate", 1), ("mhalf", NT), ("mone", NT), ("eps", NT), ("wo0", P), ("mem", DM), ("norm", 1), ("normrow", DM)]
PACK_B = [("wqk", 8 * P), ("wv", P), ("wo", P), ("band", WIN), ("bv", P), ("bo", P), ("fbias", P), ("bqk", 8),
          ("rest", 2), ("wgs", INTER), ("wds", P)]
PACK_D = [("cos", P), ("sin", P), ("nsin", P), ("fr", P), ("fi", P)]


def columns(pack):
    at, out = 0, {}
    for name, width in pack:
        out[name] = (at, at + width)
        at += width
    return out, at


COL_A, WIDTH_A = columns(PACK_A)
COL_B, WIDTH_B = columns(PACK_B)
COL_D, WIDTH_D = columns(PACK_D)

Y_BACK = 4
LN3_A, LN3_B, T3, QKV = Y_BACK + 1, Y_BACK + 5, Y_BACK + 7, Y_BACK + 8
UNITS = QKV + 4
POST = UNITS + NU + 6
PROJ, LN4_A, LN4_B, T4, FFN = POST + 2, POST + 9, POST + 13, POST + 16, POST + 19
LN1_A, LN1_B, T1, QKV0 = QKV - 2, POST - 4, POST - 1, POST + 2
CAUSAL, NUM, TCOMB, OPROJ = QKV0 + 6, QKV0 + 9, QKV0 + 11, QKV0 + 13
LN2_A, LN2_B, T2, ROUTER = OPROJ + 1, OPROJ + 5, OPROJ + 7, OPROJ + 8
CT = ROUTER + 2
LN1_A_2 = LN1_B - 5 - LN1_A
LINEAR_1 = POST - 11
X2S, KEEP, TOP = 0, 2, 3
PICK, SEL, PROB = TOP + NT, TOP + 2 * NT, TOP + 3 * NT
WEIGH = PROB + 2 * NT
GATES = WEIGH + 2
PARTS = GATES + 4
ROUTING = {TOP: 0, TOP + 1: 1, TOP + 2: 2, KEEP: Y_BACK + 2, TOP + 3: Y_BACK + 3,
           **{PICK + n: Y_BACK + 4 + n for n in range(NT)}, **{SEL + n: UNITS + 5 + n for n in range(NT)},
           **{PROB + n: POST - 6 + n for n in range(2 * NT)}, WEIGH: POST + 2,
           GATES: POST + 3, GATES + 1: POST + 4, GATES + 2: POST + 7, GATES + 3: POST + 8,
           X2S: POST + 10, X2S + 1: POST + 11, PARTS: POST + 11}
ROUTING_1 = {n: T2 - LINEAR_1 + 1 + n + max(0, min(2 * NT, n - PROB)) for n in range(PARTS + 1)}


def routing_steps(s, first):
    return [n for n, slot in (ROUTING_1 if first else ROUTING).items() if slot == s]


EARLY_SPLITS = [T1, QKV0, QKV0 + 4, QKV0 + 4, CAUSAL + 1, CAUSAL + 1, CAUSAL + 1, TCOMB, OPROJ, LN2_B, T2, ROUTER]
EARLY = len(EARLY_SPLITS)
SPLITS = [3 + 5 * n for n in range(2 * NCH - EARLY)]
assert CT < NJ - 1 and NJ % 3 == 0


QK_ORDER = (0, 1, 4, 5, 2, 3, 6, 7)


def run_batches(eng, prologue, iteration, epilogue):
    prologue()
    iteration(0, 0, False, True, True)
    with eng.Fori(0, NB // 2 - 2) as turn:
        iteration(2 * turn + 1, 1, True, True, True)
        iteration(2 * turn + 2, 0, True, True, True)
    iteration(NB - 3, 1, True, True, True)
    iteration(NB - 2, 0, True, True, False)
    iteration(NB - 1, 1, True, False, False)
    epilogue()


def window(t):
    lo, hi = max(0, P * t - HALF), min(SEQ, P * t + P + HALF)
    return lo, hi, lo - (P * t - HALF)


def chunk(t, c):
    if t == 0 and c == 0:
        return HALF, HALF
    return c * P, HALF if (t == NT - 1 and c == 1) else P


def chunk_tokens(m):
    return max(0, P * m - HALF), min(SEQ, P * m + HALF)


def heads(w):
    hp = w % (NH // 2)
    return [(4 * g + hp % 4, g, hp % 4) for g in (2 * (hp // 4), 2 * (hp // 4) + 1)]


def build(nc, x, pack_a, pack_b, pack_c, pack_d, w_up, w_down, out):
    with ExitStack() as ctx:
        def sb(name, shape, dt=F32):
            return ctx.enter_context(nc.sbuf_tensor(name, shape, dt))

        def sem(name):
            return ctx.enter_context(nc.semaphore(name))

        zp = ctx.enter_context(nc.psum_tensor("zp", [P, 2, SEQ], F32))
        gp = ctx.enter_context(nc.psum_tensor("gp", [P, 2, SEQ], F32))
        yp = ctx.enter_context(nc.psum_tensor("yp", [P, SEQ], F32))
        side = ctx.enter_context(nc.psum_tensor("side", [P, 3, SEQ], F32))

        pa = sb("pa", [P, WIDTH_A])
        pb = sb("pb", [P, WIDTH_B])
        pc = sb("pc", [P, PPG * P + P], F16)
        a = {n: pa[:, lo:hi] for n, (lo, hi) in COL_A.items()}
        c = {n: pb[:, lo:hi] for n, (lo, hi) in COL_B.items()}
        spread = pc[:, 0:PPG * P]
        identh = pc[:, PPG * P:]
        wup = sb("wup", [P, 2, NP, P], F16)
        wdn = sb("wdn", [P, 2, NP, P], F16)
        wgs, wds = sb("wgs", [P, 2, INTER], F16), sb("wds", [INTER, 2, P], F16)

        sg_gate = sb("sg_gate", [P, 4])
        flag = sb("flag", [P, 2])
        memn = sb("memn", [DM, DM + 1])
        bqk_rest = sb("bqk_rest", [P, 8])
        rT = sb("rT", [P, 2, P])
        ffn = sb("ffn", [P, P])

        x2Tn = sb("x2Tn", [P, SEQ])
        x2S = sb("x2S", [P, 2, 2, SEQ], F16)
        cT = sb("cT", [P, 2, NG, SEQ], F16)
        tb = sb("tb", [P, 3, SEQ])
        hh = sb("hh", [P, 3, 2, SEQ], F16)
        ysb = sb("ysb", [P, SEQ])

        stats = [sb(f"stats{n}", [P, NT, 6]) for n in range(4)]
        mv = [sb(f"mv{n}", [P, NT, 2]) for n in range(4)]
        ve = [sb(f"ve{n}", [P, NT]) for n in range(4)]
        rstd = [sb(f"rstd{n}", [P, NT]) for n in range(4)]
        minus = [sb(f"minus{n}", [P, NT]) for n in range(4)]
        shift = [sb(f"shift{n}", [P, NT]) for n in range(4)]
        xh01, xh23 = sb("xh01", [P, NT, P]), sb("xh23", [P, NT, P])
        xh = [xh01, xh01, xh23, xh23]

        xin = sb("xin", [P, NT, P])
        x1 = sb("x1", [P, 2, NT, P])
        xT = sb("xT", [P, SEQ])
        x1T = x3T = xT
        low, sg = sb("low", [2 * DM, SEQ]), sb("sg", [DM, 2, SEQ])
        elu = low
        va0 = sb("va0", [P, NT, DM + 1])
        at_cols = [0, SEQ, SEQ + 3 * P, SEQ + 5 * P, SEQ + 6 * P]
        qk = sb("qk", [P, 8, SEQ], F16)
        qt = sb("qt", [P, 2, SEQ], F16)
        AT = qk[:, :, :].rearrange("p a b -> p (a b)").bitcast(F32)
        dn, rc = sb("dn", [P, 8]), sb("rc", [P, 8])
        cmA, cmB, comb = sb("cmA", [P, NT, DM]), sb("cmB", [P, NT, DM]), sb("comb", [P, NT, DM])
        cbT = sb("cbT", [DM, SEQ])
        lg, key, rep, ex = (sb(n, [P, NT, NE]) for n in ("lg", "key", "rep", "ex"))
        sel = rep
        ex1 = prob = wt = cw = ex
        top = sb("top", [P, NT, 8])
        tot = sb("tot", [P, 4, NT])
        parts = sb("parts", [P, NT, NG, 2, GE], F16)

        def grouped(v):
            return v[:, :, :].rearrange("p t (g e) -> p t g e", g=NG)

        rows = sb("rows", [P, 4, NT, P])
        x2, x2b, x3, x3b = (rows[:, k] for k in range(4))
        stage = rows[:, :, :, :].rearrange("p (s a) t e -> p s (a t e)", s=2)
        vf = lg[:, :, :].rearrange("p t e -> p (t e)")[:, 0:(NT + 1) * P].rearrange("p (m e) -> p m e", e=P)
        va = sb("va", [P, NT + 1, NH, 2, HD + 1], F16)
        bvs = sb("bvs", [P, P])
        vs = sb("vs", [P, NH, HD + 1])
        sm = sb("sm", [P, 3, 2, WIN])
        pr = sm
        mn = sb("mn", [P, 3, 2])
        pT = sb("pT", [P, 3, 4, P])
        pS = sb("pS", [P, 3, 2, 4, P], F16)
        rd = sb("rd", [P, NH])
        cx = sb("cx", [P, NT, P])
        cxT = ysb
        x4T = cxT
        osb = x2

        s_a, s_b, s_c, s_d, s_x, s_out = (sem(n) for n in ("s_a", "s_b", "s_c", "s_d", "s_x", "s_out"))
        s_w = [sem(f"s_w{k}") for k in range(2)]
        s_wr, s_wl = sem("s_wr"), sem("s_wl")
        s_gate, s_memn, s_rT, s_wds = sem("s_gate"), sem("s_memn"), sem("s_rT"), sem("s_wds")
        s_f1, s_f2, s_ffnw, s_ones = sem("s_f1"), sem("s_f2"), sem("s_ffnw"), sem("s_ones")
        s_z, s_t, s_u, s_g, s_h, s_y = (sem(n) for n in ("s_z", "s_t", "s_u", "s_g", "s_h", "s_y"))
        s_hr, s_hl = sem("s_hr"), sem("s_hl")
        s_x2r, s_x2S = sem("s_x2r"), sem("s_x2S")
        f_qk, s_qt, s_qk = sem("f_qk"), sem("s_qt"), sem("s_qk")
        s_wgr = sem("s_wgr")
        s_xa, s_ex1, s_cw, s_p0, s_ysb = (sem(n) for n in ("s_xa", "s_ex1", "s_cw", "s_p0", "s_ysb"))
        s_var = [sem(f"s_var{n}") for n in range(4)]
        s_rstd = [sem(f"s_rstd{n}") for n in range(4)]
        s_xh = [sem(f"s_xh{n}") for n in range(4)]
        (f_T1, f_qk0, f_v0, f_num, f_Tcomb, f_oproj, f_T2, f_router, f_cT) = (
            sem(n) for n in ("f_T1", "f_qk0", "f_v0", "f_num", "f_Tcomb", "f_oproj", "f_T2", "f_router", "f_cT"))
        (f_Ty, f_T3, f_v, f_v4, f_Tctx, f_proj, f_T4, f_ffn) = (
            sem(n) for n in ("f_Ty", "f_T3", "f_v", "f_v4", "f_Tctx", "f_proj", "f_T4", "f_ffn"))
        (s_x1T, s_low, s_elu, s_sg, s_v0, s_comb, s_cbT, s_x1, s_x2T, s_lg, s_ex, s_prob, s_wt,
         s_parts) = (sem(n) for n in (
             "s_x1T", "s_low", "s_elu", "s_sg", "s_v0", "s_comb", "s_cbT", "s_x1", "s_x2T", "s_lg", "s_ex",
             "s_prob", "s_wt", "s_parts"))
        (s_x2, s_x2b, s_x3T, s_v, s_v4, s_cxT, s_x3, s_x3b, s_x4T, s_o) = (sem(n) for n in (
            "s_x2", "s_x2b", "s_x3T", "s_v", "s_v4", "s_cxT", "s_x3", "s_x3b", "s_x4T", "s_o"))
        f_AT, s_ATd, s_ATc, s_cT = sem("f_AT"), sem("s_ATd"), sem("s_ATc"), sem("s_cT")
        f_sc, s_sm, s_pr, f_pT, s_pT = sem("f_sc"), sem("s_sm"), sem("s_pr"), sem("f_pT"), sem("s_pT")
        s_pr2, s_pl = sem("s_pr2"), sem("s_pl")
        s_vr, s_vl = sem("s_vr"), sem("s_vl")
        f_pv, s_vs, s_cx = sem("f_pv"), sem("s_vs"), sem("s_cx")

        pd = qk[:, :, :].rearrange("p a b -> p (a b)").bitcast(F32)[:, 0:WIDTH_D]
        d = {n: pd[:, lo:hi] for n, (lo, hi) in COL_D.items()}

        xv = x.rearrange("b (t p) h -> b p t h", p=P)
        ov = out.rearrange("b (t p) h -> b p t h", p=P)

        def heads_of(v):
            return v[:, :, :].rearrange("p m (h e) -> p m h e", h=NH)

        def last_batch(b):
            return isinstance(b, int) and b == NB - 1

        def at_zero(b):
            return isinstance(b, int) and b == 0

        def context_slot(b):
            return 6 if last_batch(b) else 5

        def scores_bank(b, w):
            return gp[:, 0, :] if last_batch(b) and w % 2 else side[:, 0, :]

        def probs_bank(b, w):
            return gp[:, 1, :] if last_batch(b) and w % 2 else side[:, 1, :]

        def qk_bank(b, p):
            if last_batch(b):
                first = [side[:, 0, :], side[:, 2, :], zp[:, 0, :], zp[:, 1, :]]
                return first[p] if p < 4 else first[1 + (p - 4) % 3], (0 if p < 4 else p - 2)
            return side[:, (0, 2, 0, 2, 1, 2, 1, 2)[p], :], max(0, p - 1)

        block = ctx.enter_context(nc.Block())

        @block.sync
        def _(sp):
            def load_x(b):
                if not at_zero(b):
                    sp.wait_ge(s_x1, b)
                sp.dma_start(xin[:, :, :], xv[b]).then_inc(s_x, 16)

            load_x(0)
            sp.dma_start(pa[:, :], pack_a).then_inc(s_a, 16)
            sp.dma_start(pd, pack_d).then_inc(s_d, 16)
            sp.dma_start(pc[:, :], pack_c).then_inc(s_c, 16)
            sp.dma_start(pb[:, :], pack_b).then_inc(s_b, 16)
            for n in range(2 * NCH):
                k, src = n // 2, (w_up, w_down)[n % 2]
                if n == EARLY + 2:
                    load_x(1)
                if n >= 2:
                    sp.wait_ge(s_wl, n - 1)
                sp.dma_start(stage[:, n % 2, :], src[:, k * CH * P:(k + 1) * CH * P]).then_inc(s_w[n % 2], 16)

            def iteration(i, par, before, after, ahead):
                if ahead:
                    load_x(i + 2)
                if before:
                    sp.wait_ge(s_o, i)
                    sp.dma_start(ov[i - 1], osb[:, :, :]).then_inc(s_out, 16)

            def epilogue():
                sp.wait_ge(s_o, NB)
                sp.dma_start(ov[NB - 1], osb[:, :, :]).then_inc(s_out, 16)
                sp.wait_ge(s_out, 16 * NB)

            run_batches(sp, lambda: None, iteration, epilogue)

        @block.tensor
        def _(pe):
            def transposes(bank, src):
                for t in range(NT):
                    last = pe.transpose(side[:, bank, t * P:(t + 1) * P], src(t), a["ident"])
                return last

            def setup():
                pe.wait_ge(s_d, 16)
                for k, (p1, p2, s2) in enumerate((("fr", "fi", "sin"), ("fi", "fr", "nsin"))):
                    pe.matmul(side[:, 1, k * P:(k + 1) * P], d[p1], d["cos"], start=True, stop=False)
                    last = pe.matmul(side[:, 1, k * P:(k + 1) * P], d[p2], d[s2], start=False, stop=True)
                last.then_inc(s_f1, 1)
                pe.wait_ge(s_rT, 1)
                pe.matmul(side[:, 1, 2 * P:3 * P], rT[:, 0, :], d["cos"], start=True, stop=False)
                pe.matmul(side[:, 1, 2 * P:3 * P], rT[:, 1, :], d["nsin"], start=False, stop=True).then_inc(s_f2, 1)
                pe.wait_ge(s_ffnw, 1)

            def l0_T1(b, before):
                pe.wait_ge(s_xh[0], b + 1)
                if before:
                    pe.wait_ge(s_vs, NT * (b - 2))
                transposes(2, lambda t: xh[0][:, t, :]).then_inc(f_T1, 1)

            def l0_qkv(b, before):
                pe.wait_ge(s_x1T, b + 1)
                if before:
                    pe.wait_ge(s_cxT, b - 2)
                elif b > 0:
                    pe.wait_ge(s_lg, b)
                    pe.wait_ge(s_cT, NG // 2)
                pe.matmul(side[0:2 * DM, 0, :], a["wqk0"], x1T[:, :], start=True, stop=True).then_inc(f_qk0, 1)
                for t in range(NT):
                    last = pe.matmul(side[:, 2, t * DM:(t + 1) * DM], x1T[:, t * P:(t + 1) * P], a["wv0"],
                                     start=True, stop=True)
                last.then_inc(f_v0, 1)

            def l0_causal(b, before):
                if before:
                    pe.wait_ge(s_x3, b - 2)
                pe.wait_ge(s_sg, 2 * b + 2)
                pe.wait_ge(s_v0, b + 1)
                for bank, kts in enumerate(((0,), (1,), (2, 3))):
                    for kt in kts:
                        at = at_cols[kt] - at_cols[kts[0]]
                        n = SEQ - kt * P
                        last = pe.matmul(side[:, bank, at:at + n], sg[:, 1, kt * P:(kt + 1) * P], sg[:, 0, kt * P:],
                                         start=True, stop=True)
                    last.then_inc(f_AT, 1)

            def l0_num(b, tiles):
                w = DM + 1
                if tiles[0] == 0:
                    pe.wait_ge(s_ATc, 3 * b + 3)
                    pe.wait_ge(s_ATd, 4 * b + 4)
                for qt in tiles:
                    for kt in range(qt + 1):
                        at = at_cols[kt] + (qt - kt) * P
                        pe.matmul(side[:, 0, qt * w:(qt + 1) * w], AT[:, at:at + P], va0[:, kt, :],
                                  start=(kt == 0), stop=(kt == qt))
                if tiles[-1] == NT - 1:
                    for qt in range(NT):
                        last = pe.matmul(side[:, 0, (NT + qt) * w:(NT + qt + 1) * w], sg[:, 0, qt * P:(qt + 1) * P],
                                         memn[:, :], start=True, stop=True)
                    last.then_inc(f_num, 1)

            def l0_Tcomb(b):
                pe.wait_ge(s_comb, b + 1)
                for t in range(NT):
                    last = pe.transpose(side[0:DM, 1, t * P:(t + 1) * P], comb[:, t, :], a["ident"])
                last.then_inc(f_Tcomb, 1)

            def l0_oproj(b):
                pe.wait_ge(s_cbT, b + 1)
                for t in range(NT):
                    last = pe.matmul(side[:, 0, t * P:(t + 1) * P], cbT[:, t * P:(t + 1) * P], a["wo0"][0:DM],
                                     start=True, stop=True)
                last.then_inc(f_oproj, 1)

            def l0_T2(b):
                pe.wait_ge(s_xh[1], b + 1)
                transposes(1, lambda t: xh[1][:, t, :]).then_inc(f_T2, 1)

            def l0_router(b):
                pe.wait_ge(s_x2T, b + 1)
                for t in range(NT):
                    last = pe.matmul(side[:, t // 2, (t % 2) * NE:(t % 2 + 1) * NE], x2Tn[:, t * P:(t + 1) * P],
                                     a["router"], start=True, stop=True)
                last.then_inc(f_router, 1)

            def l0_cT(b, logits):
                pe.wait_ge(s_parts, b + 1)
                pe.wait_ge(s_lg, logits)
                for g in range(NG):
                    bank = side[:, g // 2, :].bitcast(F16)
                    for t in range(NT):
                        at = (g % 2) * SEQ + t * P
                        last = pe.transpose(bank[0:2 * GE, at:at + P],
                                            parts[:, t, g, :, :].rearrange("p k e -> p (k e)"), identh)
                    if g % 2:
                        last.then_inc(f_cT, 1)

            def l1_Ty(b, gates):
                pe.wait_ge(s_ysb, b + 1)
                pe.wait_ge(s_cT, NG // 2 * gates)
                if last_batch(b):
                    pe.wait_ge(s_o, b)
                transposes(0, lambda t: ysb[:, t * P:(t + 1) * P]).then_inc(f_Ty, 1)

            def l1_T3(b):
                pe.wait_ge(s_xh[2], b + 1)
                transposes(1, lambda t: xh[2][:, t, :]).then_inc(f_T3, 1)

            def l1_qk(b, p):
                if p == 0:
                    pe.wait_ge(s_x3T, b + 1)
                bank, free = qk_bank(b, p)
                if free > 0:
                    pe.wait_ge(s_qk, 8 * b + free)
                if p == 4:
                    pe.wait_ge(s_v4, b + 1)
                m = QK_ORDER[p]
                pe.matmul(bank, c["wqk"][:, m * P:(m + 1) * P], x3T[:, :], start=True, stop=True).then_inc(f_qk, 1)

            def l1_v(b):
                for m in range(NT):
                    lo, hi = chunk_tokens(m)
                    last = pe.matmul(side[0:hi - lo, 1, m * P:(m + 1) * P], x3T[:, lo:hi], c["wv"],
                                     start=True, stop=True)
                last.then_inc(f_v, 1)

            def l1_v4(b):
                pe.wait_ge(s_v, b + 1)
                lo, hi = chunk_tokens(NT)
                pe.matmul(side[0:hi - lo, 1, 0:P], x3T[:, lo:hi], c["wv"], start=True, stop=True).then_inc(f_v4, 1)

            def scores(b, w):
                t = w // (NH // 2)
                lo, hi, off = window(t)
                if w == 0 or w == NH // 4:
                    pe.wait_ge(s_qk, 8 * b + (4 if w == 0 else 8))
                if w == 0:
                    pass
                elif last_batch(b) and w > 1:
                    pe.wait_ge(s_sm, NU * b + w - 1)
                elif not last_batch(b):
                    pe.wait_ge(s_sm, NU * b + w)
                for k, (_, g, r) in enumerate(heads(w)):
                    last = pe.matmul(scores_bank(b, w)[:, k * WIN + off:k * WIN + off + hi - lo],
                                     qk[32 * r:32 * r + 32, g, t * P:(t + 1) * P], qk[32 * r:32 * r + 32, 4 + g, lo:hi],
                                     start=True, stop=True)
                last.then_inc(f_sc, 1)

            def turn_probs(b, w):
                t = w // (NH // 2)
                pe.wait_ge(s_pr, NU * b + w + 1)
                if w == 0:
                    pe.wait_ge(s_qk, 8 * b + 7)
                elif last_batch(b) and w > 1:
                    pe.wait_ge(s_pT, NU * b + w - 1)
                elif not last_batch(b):
                    pe.wait_ge(s_pT, NU * b + w)
                for k in range(2):
                    for cc in ((1, 0) if t == 0 else (0, 1)):
                        col, rows = chunk(t, cc)
                        last = pe.transpose(probs_bank(b, w)[0:rows, (2 * k + cc) * P:(2 * k + cc + 1) * P],
                                            pr[:, w % 3, k, col:col + rows], a["ident"])
                last.then_inc(f_pT, 1)

            def context(b, w):
                t, hp = w // (NH // 2), w % (NH // 2)
                pe.wait_ge(s_pl, NU * b + w + 1)
                if w == 0:
                    pe.wait_ge(s_vl, b + 1)
                if hp == 0 and t > 0:
                    pe.wait_ge(s_vs, NT * b + t)
                for k, (h, _, _) in enumerate(heads(w)):
                    for cc in range(2):
                        _, rows = chunk(t, cc)
                        for part in range(2):
                            last = pe.matmul(side[:, 2, h * VW:(h + 1) * VW], pS[0:rows, w % 3, part, 2 * k + cc, :],
                                             va[0:rows, t + cc, h, :, :].rearrange("p k e -> p (k e)"),
                                             start=(cc == 0 and part == 0), stop=(cc == 1 and part == 1))
                last.then_inc(f_pv, 1)

            def l1_Tctx(b):
                pe.wait_ge(s_cx, NT * b + NT)
                pe.wait_ge(s_sm, NU * b + NU)
                transposes(0, lambda t: cx[:, t, :]).then_inc(f_Tctx, 1)

            def project(f_sem, bank, srcT, w):
                for t in range(NT):
                    last = pe.matmul(side[:, bank, t * P:(t + 1) * P], srcT[:, t * P:(t + 1) * P], w,
                                     start=True, stop=True)
                last.then_inc(f_sem, 1)

            def l1_proj(b):
                pe.wait_ge(s_cxT, b + 1)
                pe.wait_ge(s_pT, NU * b + NU)
                project(f_proj, 1, cxT, c["wo"])

            def l1_T4(b):
                pe.wait_ge(s_xh[3], b + 1)
                transposes(2, lambda t: xh[3][:, t, :]).then_inc(f_T4, 1)

            def l1_ffn(b):
                pe.wait_ge(s_x4T, b + 1)
                project(f_ffn, 2, x4T, ffn[:, :])

            def three_passes(acc, w, v, start, stop):
                pe.matmul(acc, w(0), v(0), start=start, stop=False)
                pe.matmul(acc, w(0), v(1), start=False, stop=False)
                return pe.matmul(acc, w(1), v(0), start=False, stop=stop)

            def up(i, par, j, before):
                if j == 0:
                    pe.wait_ge(s_x2S, i + 1)
                if before or j >= 2:
                    pe.wait_ge(s_u, NJ * i + j - 1)
                n, w = (P, lambda k: wup[:, k, j, :]) if j < NP else (INTER, lambda k: wgs[:, k, :])
                three_passes(zp[0:n, (par + j) % 2, :], w, lambda k: x2S[:, par, k, :], True, True).then_inc(s_z, 1)

            def gates(i, par, j, before):
                if j == 0:
                    pe.wait_ge(s_cT, NG // 2 * (i + 1))
                if before or j >= 2:
                    pe.wait_ge(s_h, NJ * i + j - (1 if j >= 2 else 2))
                g, u = j // PPG, j % PPG
                pe.matmul(gp[:, j % 2, :], spread[0:2 * GE, u * P:(u + 1) * P], cT[0:2 * GE, par, g, :],
                          start=True, stop=True).then_inc(s_g, 1)

            def down(i, j):
                if j == 0 and not at_zero(i):
                    pe.wait_ge(s_ysb, i)
                pe.wait_ge(s_hl, NJ * i + j + 1)
                n, w = (P, lambda k: wdn[:, k, j, :]) if j < NP else (INTER, lambda k: wds[:, k, :])
                three_passes(yp[:, :], w, lambda k: hh[0:n, j % 3, k, :], j == 0, j == NP).then_inc(s_y, 1)

            def banded(b, s, g):
                w = s - UNITS
                if s == Y_BACK:
                    l1_Ty(b, g)
                if s == T3:
                    l1_T3(b)
                if QKV <= s < QKV + 8:
                    l1_qk(b, s - QKV)
                if s == QKV:
                    l1_v(b)
                if s == QKV + 1:
                    l1_v4(b)
                if 0 <= w - 3 < NU:
                    turn_probs(b, w - 3)
                if s == POST:
                    l1_Tctx(b)
                if s == PROJ:
                    l1_proj(b)
                if s == T4:
                    l1_T4(b)
                if s == FFN:
                    l1_ffn(b)

            def late(b, s):
                if last_batch(b) and 0 <= s - UNITS < NU:
                    scores(b, s - UNITS)
                if 0 <= s - UNITS - context_slot(b) < NU:
                    context(b, s - UNITS - context_slot(b))
                if not last_batch(b) and 0 <= s - UNITS < NU:
                    scores(b, s - UNITS)

            def linear(b, s, before):
                if s == T1:
                    l0_T1(b, before)
                if s == QKV0:
                    l0_qkv(b, before)
                if s == CAUSAL:
                    l0_causal(b, before)
                if s == NUM:
                    l0_num(b, range(NT - 1))
                if s == NUM + 1:
                    l0_num(b, range(NT - 1, NT))
                if s == TCOMB:
                    l0_Tcomb(b)
                if s == OPROJ:
                    l0_oproj(b)
                if s == T2:
                    l0_T2(b)
                if s == ROUTER:
                    l0_router(b)

            def iteration(i, par, before, after, ahead):
                for s in range(NJ):
                    if not before and s == NP:
                        pe.wait_ge(s_wds, 1)
                    if not before and s % CH == 0 and s < NP:
                        pe.wait_ge(s_wl, 2 * (s // CH) + 2)
                    up(i, par, s, before)
                    if s < NP:
                        gates(i, par, s, before)
                    if before:
                        banded(i - 1, s, i + 1)
                    if not before:
                        linear(1, s + LINEAR_1, False)
                    if ahead:
                        linear(i + 2, s, before)
                    if after and s == CT:
                        l0_cT(i + 1, i + 3 if ahead else i + 2)
                    if s == 4:
                        down(i, 0)
                    if s >= 4:
                        down(i, s - 3)
                    elif s < 3 and before:
                        down(i - 1, NJ - 3 + s)
                    if before:
                        late(i - 1, s)

            def prologue():
                pe.wait_ge(s_a, 16)
                pe.wait_ge(s_memn, 1)
                pe.wait_ge(s_ones, 1)
                for s in range(NJ):
                    linear(0, s, False)
                    if s == QKV0:
                        setup()
                pe.wait_ge(s_c, 16)
                l0_cT(0, 1)

            def epilogue():
                for j in range(NJ - 3, NJ):
                    down(NB - 1, j)
                for s in range(NJ):
                    banded(NB - 1, s, NB)
                    late(NB - 1, s)

            run_batches(pe, prologue, iteration, epilogue)

        @block.scalar
        def _(act):
            def setup():
                act.wait_ge(s_a, 16)
                act.activation(sg_gate[:, 0:1], a["gate"], ACT.Exp, scale=-1.0).then_inc(s_gate, 1)

            def feed_forward_matrix():
                act.wait_ge(s_f1, 1)
                act.activation(rT[:, :, :], side[:, 1, 0:2 * P].rearrange("p (k e) -> p k e", k=2),
                               ACT.Copy).then_inc(s_rT, 1)
                act.wait_ge(s_f2, 1)
                act.activation(ffn[:, :], side[:, 1, 2 * P:3 * P], ACT.Copy, scale=1.0 / H).then_inc(s_ffnw, 1)

            def norm_apply(n, src, b, half):
                if half == 0:
                    act.wait_ge(s_rstd[n], b + 1)
                for t in (2 * half, 2 * half + 1):
                    last = act.activation(xh[n][:, t, :], src[:, t, :], ACT.Identity, scale=rstd[n][:, t:t + 1],
                                          bias=shift[n][:, t:t + 1])
                if half == 1:
                    last.then_inc(s_xh[n], 1)

            def out_of_psum(dst, bank, full, value, done):
                act.wait_ge(full, value)
                act.activation(dst, side[:, bank, :], ACT.Copy).then_inc(done, 1)

            def linear(b, s):
                if s in (LN1_B, LN1_B + 1):
                    norm_apply(0, xin, b, s - LN1_B)
                if s in (LN2_B, LN2_B + 1):
                    norm_apply(1, xin, b, s - LN2_B)
                if s == T1:
                    out_of_psum(x1T[:, :], 2, f_T1, b + 1, s_x1T)
                if s == QKV0:
                    act.wait_ge(f_v0, b + 1)
                    act.activation(va0[:, :, 0:DM], side[:, 2, 0:NT * DM].rearrange("p (t e) -> p t e", t=NT),
                                   ACT.Copy).then_inc(s_v0, 1)
                if s == QKV0 + 1:
                    act.wait_ge(f_qk0, b + 1)
                    act.activation(low[:, :], side[0:2 * DM, 0, :], ACT.Relu, scale=-1.0).then_inc(s_low, 1)
                if s == QKV0 + 2:
                    act.wait_ge(s_low, b + 1)
                    act.activation(elu[:, :], low[:, :], ACT.Exp, scale=-1.0).then_inc(s_elu, 1)
                if s == CAUSAL + 1:
                    for bank, kt in enumerate((0, 1, 2)):
                        act.wait_ge(s_ATd, 4 * b + (1, 2, 4)[bank])
                        act.activation(AT[:, at_cols[kt] + P:at_cols[kt + 1]],
                                       side[:, bank, P:SEQ - kt * P], ACT.Copy).then_inc(s_ATc, 1)
                if s == TCOMB:
                    act.wait_ge(f_Tcomb, b + 1)
                    act.activation(cbT[:, :], side[0:DM, 1, :], ACT.Copy).then_inc(s_cbT, 1)
                if s == T2:
                    out_of_psum(x2Tn[:, :], 1, f_T2, b + 1, s_x2T)
                if s == ROUTER + 1:
                    act.wait_ge(s_lg, b + 1)
                    act.activation(ex[:, :, :], lg[:, :, :], ACT.Exp, scale=-1.0).then_inc(s_ex, 1)
                if s == ROUTER + 2:
                    act.wait_ge(s_ex, b + 1)
                    act.activation(ex1[:, :, :], ex[:, :, :], ACT.Copy, bias=1.0).then_inc(s_ex1, 1)

            def routing(b, par, s, before):
                for step in routing_steps(s, not before):
                    routing_step(b, par, step, before)
                if s == CT:
                    for k in range(NG // 2):
                        act.wait_ge(f_cT, NG // 2 * b + k + 1)
                        act.activation(cT[0:2 * GE, par, 2 * k:2 * k + 2, :].rearrange("p g t -> p (g t)"),
                                       side[0:2 * GE, k, :].bitcast(F16), ACT.Copy).then_inc(s_cT, 1)

            def routing_step(b, par, s, before):
                if s == KEEP:
                    act.wait_ge(s_xa, b + 1)
                    if before:
                        act.wait_ge(s_x2, b - 1)
                    act.activation(x1[:, par], xin[:, :, :], ACT.Copy).then_inc(s_x1, 1)
                if s == X2S:
                    act.wait_ge(s_x2T, b + 1)
                    act.activation(x2S[:, par, 0, :], x2Tn[:, :], ACT.Copy).then_inc(s_x2r, 1)
                if s == GATES + 3:
                    act.wait_ge(s_cw, b + 1)
                    act.activation(parts[:, :, :, 0, :], grouped(cw), ACT.Copy).then_inc(s_p0, 1)

            def banded(b, s):
                w = s - UNITS
                if s in (LN3_B, LN3_B + 1):
                    norm_apply(2, x2, b, s - LN3_B)
                if s in (LN4_B, LN4_B + 1):
                    norm_apply(3, x3, b, s - LN4_B)
                if s == T3:
                    out_of_psum(x3T[:, :], 1, f_T3, b + 1, s_x3T)
                if QKV <= s < QKV + 8:
                    p = s - QKV
                    m = QK_ORDER[p]
                    act.wait_ge(f_qk, 8 * b + p + 1)
                    if p >= 2:
                        act.wait_ge(s_qk, 8 * b + p - 1)
                    act.activation(qt[:, p % 2, :], qk_bank(b, p)[0], ACT.Identity,
                                   scale=c["rest"][:, m // 4:m // 4 + 1], bias=bqk_rest[:, m:m + 1]).then_inc(s_qt, 1)
                if last_batch(b) and 0 <= w - 3 < NU:
                    probs(b, w - 3)
                if 0 <= w - 1 < NU:
                    exps(b, w - 1)
                if not last_batch(b) and 0 <= w - 3 < NU:
                    probs(b, w - 3)
                if s == POST:
                    out_of_psum(cxT[:, :], 0, f_Tctx, b + 1, s_cxT)
                if s == T4:
                    out_of_psum(x4T[:, :], 2, f_T4, b + 1, s_x4T)

            def exps(b, w):
                lo, hi, off = window(w // (NH // 2))
                act.wait_ge(s_sm, NU * b + w + 1)
                for k in range(2):
                    last = act.activation(pr[:, w % 3, k, off:off + hi - lo], sm[:, w % 3, k, off:off + hi - lo],
                                          ACT.Exp, scale=-1.0, bias=mn[:, w % 3, k:k + 1])
                last.then_inc(s_pr, 1)

            def probs(b, w):
                t = w // (NH // 2)
                act.wait_ge(f_pT, NU * b + w + 1)
                src = probs_bank(b, w).rearrange("p (k q) -> p k q", k=4)
                if w >= 3:
                    act.wait_ge(s_pl, NU * b + w - 2)
                if 0 < t < NT - 1:
                    act.activation(pT[:, w % 3, :, :], src, ACT.Copy, scale=PS).then_inc(s_pT, 1)
                    return
                for cc in range(2):
                    _, rows = chunk(t, cc)
                    last = act.activation(pT[0:rows, w % 3, cc::2, :], src[0:rows, cc::2, :], ACT.Copy, scale=PS)
                last.then_inc(s_pT, 1)

            def rounded(i, j):
                n = P if j < NP else INTER
                act.wait_ge(s_h, NJ * i + j + 1)
                if j >= 3 or not at_zero(i):
                    act.wait_ge(s_y, NJ * i + j - 2)
                act.activation(hh[0:n, j % 3, 0, :], tb[0:n, j % 3, :], ACT.Copy).then_inc(s_hr, 1)

            def iteration(i, par, before, after, ahead):
                for s in range(NJ):
                    if s == 3 and before:
                        act.wait_ge(s_y, NJ * i)
                        act.activation(ysb[:, :], yp[:, :], ACT.Copy, scale=1.0 / WS).then_inc(s_ysb, 1)
                    n = P if s < NP else INTER
                    act.wait_ge(s_z, NJ * i + s + 1)
                    if before or s >= 3:
                        act.wait_ge(s_hl, NJ * i + s - 2)
                    act.activation(tb[0:n, s % 3, :], zp[0:n, (par + s) % 2, :], ACT.Tanh,
                                   scale=0.5 / WS).then_inc(s_t, 1)
                    if s >= 1:
                        rounded(i, s - 1)
                    elif before:
                        rounded(i - 1, NJ - 1)
                    if before:
                        banded(i - 1, s)
                    if not before:
                        linear(1, s + LINEAR_1)
                        split_beside(s)
                    if after:
                        routing(i + 1, 1 - par, s, before)
                    if ahead:
                        linear(i + 2, s)

            def split(n):
                k, dst = n // 2, (wup, wdn)[n % 2]
                act.wait_ge(s_w[n % 2], 16 * (n // 2 + 1))
                act.activation(dst[:, 0, k * CH:(k + 1) * CH, :], stage[:, n % 2, :].rearrange(
                    "p (j e) -> p j e", j=CH), ACT.Copy, scale=WS).then_inc(s_wr, 1)

            def split_beside(s):
                if s in SPLITS:
                    split(EARLY + SPLITS.index(s))

            def prologue():
                setup()
                for s in range(NJ):
                    linear(0, s)
                    if s == QKV0 + 2:
                        feed_forward_matrix()
                    for n, slot in enumerate(EARLY_SPLITS):
                        if slot == s:
                            split(n)
                for s in range(NJ):
                    routing(0, 0, s, False)
                act.wait_ge(s_b, 16)
                act.activation(wgs[:, 0, :], c["wgs"], ACT.Copy, scale=WS)
                act.activation(wds[:, 0, :], c["wds"][0:INTER], ACT.Copy, scale=WS).then_inc(s_wgr, 1)

            def epilogue():
                rounded(NB - 1, NJ - 1)
                act.wait_ge(s_y, NJ * NB)
                act.activation(ysb[:, :], yp[:, :], ACT.Copy, scale=1.0 / WS).then_inc(s_ysb, 1)
                for s in range(NJ):
                    banded(NB - 1, s)

            run_batches(act, prologue, iteration, epilogue)

        @block.vector
        def _(dve):
            def link(ins, wait=True):
                if wait:
                    dve.drain()

            def setup():
                dve.memset(va0[:, :, DM:DM + 1], 1.0).then_inc(s_ones, 1)
                for s in range(NJ):
                    take_up(0, s)
                dve.wait_ge(s_a, 16)
                dve.wait_ge(s_gate, 1)
                link(dve.tensor_scalar(sg_gate[:, 1:2], sg_gate[:, 0:1], 1.0, None, ALU.add))
                link(dve.reciprocal(sg_gate[:, 2:3], sg_gate[:, 1:2]))
                link(dve.tensor_scalar(sg_gate[:, 3:4], sg_gate[:, 2:3], -1.0, 1.0, ALU.mult, ALU.add))
                link(dve.tensor_reduce(flag[:, 0:1], a["normrow"], AX.X, ALU.add))
                link(dve.tensor_scalar(flag[:, 1:2], flag[:, 0:1], EPS, None, ALU.is_ge))
                link(dve.tensor_scalar(memn[:, 0:DM], a["mem"][0:DM], sg_gate[0:DM, 2:3], flag[0:DM, 1:2],
                                       ALU.mult, ALU.mult))
                dve.tensor_copy(memn[:, DM:DM + 1], a["norm"][0:DM]).then_inc(s_memn, 1)

            def rest(dst, src):
                return dve.scalar_tensor_tensor(dst(1), src, WS, dst(0), ALU.mult, ALU.subtract)

            def late_setup():
                dve.memset(pT[:, :, :, :], 0.0)
                dve.memset(va[:, :, :, 0, HD:HD + 1], WS)
                dve.memset(va[:, :, :, 1, HD:HD + 1], 0.0)
                dve.wait_ge(s_b, 16)
                dve.tensor_scalar(bvs[:, :], c["bv"], WS, None, ALU.mult)
                for k in range(2):
                    last = dve.tensor_scalar(bqk_rest[:, 4 * k:4 * k + 4], c["bqk"][:, 4 * k:4 * k + 4],
                                             c["rest"][:, k:k + 1], None, ALU.mult)
                dve.wait_ge(s_wgr, 1)
                rest(lambda k: wgs[:, k, :], c["wgs"])
                rest(lambda k: wds[:, k, :], c["wds"][0:INTER]).then_inc(s_wds, 1)

            def split(n):
                k, dst = n // 2, (wup, wdn)[n % 2]
                dve.wait_ge(s_wr, n + 1)
                rest(lambda q: dst[:, q, k * CH:(k + 1) * CH, :],
                     stage[:, n % 2, :].rearrange("p (j e) -> p j e", j=CH)).then_inc(s_wl, 1)

            def split_beside(s):
                if s in SPLITS:
                    split(EARLY + SPLITS.index(s))

            def norm_stats(n, src, half):
                for t in (2 * half, 2 * half + 1):
                    link(dve.bn_stats(stats[n][:, t, :], src[:, t, :]), wait=(half == 1 and t == NT - 1))
                if half == 1:
                    for t in range(NT):
                        last = dve.bn_aggr(mv[n][:, t, :], stats[n][:, t, :])
                    last.then_inc(s_var[n], 1)

            def tiles(ap):
                return ap.rearrange("p (t e) -> p t e", t=NT)

            def take_up(b, s):
                if s in (LN1_A, LN1_A + 1):
                    if s == LN1_A:
                        dve.wait_ge(s_x, 16 * b + 16)
                    norm_stats(0, xin, s - LN1_A)

            def linear(b, s):
                if s in (QKV0 + 3, QKV0 + 4):
                    n = s - QKV0 - 3
                    if n == 0:
                        dve.wait_ge(s_elu, b + 1)
                    strip = slice(n * DM, (n + 1) * DM)
                    dve.scalar_tensor_tensor(sg[:, n, :], side[strip, 0, :], 0.0, elu[strip, :], ALU.max,
                                             ALU.add).then_inc(s_sg, 1)
                if s == CAUSAL:
                    for bank, kt in ((0, 0), (1, 1), (2, 2), (2, 3)):
                        dve.wait_ge(f_AT, 3 * b + bank + 1)
                        at = 2 * P if kt == 3 else 0
                        dve.tensor_tensor(AT[:, at_cols[kt]:at_cols[kt] + P], side[:, bank, at:at + P], a["causal"],
                                          ALU.mult).then_inc(s_ATd, 1)
                if s == NUM + 1:
                    dve.wait_ge(f_num, b + 1)
                    v = side[:, 0, 0:8 * (DM + 1)].rearrange("p (m e) -> p m e", m=8)
                    link(dve.tensor_scalar(dn[:, :].unsqueeze(2), v[:, :, DM:DM + 1], EPS, None, ALU.max))
                    link(dve.reciprocal(rc[:, :], dn[:, :]))
                    link(dve.tensor_scalar(rc[:, 0:NT], rc[:, 0:NT], sg_gate[:, 3:4], None, ALU.mult))
                    for dst, lo in ((cmA, 0), (cmB, NT)):
                        link(dve.tensor_tensor(dst[:, :, :], v[:, lo:lo + NT, 0:DM],
                                               rc[:, lo:lo + NT].unsqueeze(2).to_broadcast([P, NT, DM]), ALU.mult),
                             wait=(lo == NT))
                    dve.tensor_tensor(comb[:, :, :], cmA[:, :, :], cmB[:, :, :], ALU.add).then_inc(s_comb, 1)
                if s == OPROJ:
                    dve.wait_ge(f_oproj, b + 1)
                    dve.tensor_tensor(xin[:, :, :], tiles(side[:, 0, :]), xin[:, :, :], ALU.add).then_inc(s_xa, 1)
                if s in (LN2_A, LN2_A + 1):
                    if s == LN2_A:
                        dve.wait_ge(s_xa, b + 1)
                    norm_stats(1, xin, s - LN2_A)
                if s == ROUTER:
                    dve.wait_ge(f_router, b + 1)
                    dve.tensor_tensor(lg[:, :, :].rearrange("p (u v) e -> p u (v e)", u=2), side[:, 0:2, 0:2 * NE],
                                      a["ebias"].unsqueeze(1).to_broadcast([P, 2, 2 * NE]), ALU.add).then_inc(s_lg, 1)
                if s == ROUTER + 2:
                    dve.wait_ge(s_lg, b + 1)
                    link(dve.tensor_scalar(key[:, :, :], lg[:, :, :], SAT, -87.0, ALU.min, ALU.max))

            def routing(b, par, s, before):
                for step in routing_steps(s, not before):
                    routing_step(b, par, step)

            def routing_step(b, par, s):
                if s == X2S + 1:
                    dve.wait_ge(s_x2r, b + 1)
                    dve.tensor_tensor(x2S[:, par, 1, :], x2Tn[:, :], x2S[:, par, 0, :], ALU.subtract).then_inc(s_x2S, 1)
                t = (s - TOP) % NT
                if TOP <= s < PICK:
                    link(dve.max(top[:, t, :], key[:, t, :]))
                if PICK <= s < SEL:
                    link(dve.match_replace(rep[:, t, :], top[:, t, :], key[:, t, :], -BIG))
                if SEL <= s < PROB:
                    dve.tensor_tensor(sel[:, t, :], rep[:, t, :], key[:, t, :], ALU.not_equal)
                if PROB <= s < WEIGH:
                    if s == PROB:
                        dve.wait_ge(s_ex1, b + 1)
                    t, half = (s - PROB) // 2, (s - PROB) % 2
                    cols = slice(half * NE // 2, (half + 1) * NE // 2)
                    dve.reciprocal(prob[:, t, cols], ex1[:, t, cols]).then_inc(s_prob, 1)
                if s == GATES:
                    dve.wait_ge(s_wt, b + 1)
                    link(dve.tensor_reduce(tot[:, 0, :], wt[:, :, :], AX.X, ALU.add))
                if s == GATES + 1:
                    link(dve.tensor_scalar(tot[:, 1, :], tot[:, 0, :], GATE_EPS, None, ALU.add))
                    link(dve.reciprocal(tot[:, 2, :], tot[:, 1, :]))
                    link(dve.tensor_scalar(tot[:, 3, :], tot[:, 2, :], GS * ROUTED_SCALE / 2 / WS, None, ALU.mult))
                if s == GATES + 2:
                    dve.tensor_tensor(cw[:, :, :], wt[:, :, :], tot[:, 3, :].unsqueeze(2).to_broadcast([P, NT, NE]),
                                      ALU.mult).then_inc(s_cw, 1)
                if s == PARTS:
                    dve.wait_ge(s_p0, b + 1)
                    dve.tensor_tensor(parts[:, :, :, 1, :], grouped(cw), parts[:, :, :, 0, :],
                                      ALU.subtract).then_inc(s_parts, 1)

            def banded(b, par, s):
                w = s - UNITS
                if s == Y_BACK:
                    dve.wait_ge(f_Ty, b + 1)
                    dve.wait_ge(s_x1, b + 1)
                    dve.tensor_tensor(x2[:, :, :], tiles(side[:, 0, :]), x1[:, par], ALU.add).then_inc(s_x2, 1)
                if s in (LN3_A, LN3_A + 1):
                    if s == LN3_A:
                        dve.wait_ge(s_x2, b + 1)
                    norm_stats(2, x2, s - LN3_A)
                if QKV <= s < QKV + 8:
                    p = s - QKV
                    m = QK_ORDER[p]
                    dve.wait_ge(s_qt, 8 * b + p + 1)
                    dve.scalar_tensor_tensor(qk[:, m, :], qk_bank(b, p)[0], c["bqk"][:, m:m + 1], qt[:, p % 2, :],
                                             ALU.add, ALU.subtract).then_inc(s_qk, 1)
                if s == QKV:
                    dve.wait_ge(f_v, b + 1)
                    for m in range(NT):
                        last = values(m, 1, m * P)
                    last.then_inc(s_v, 1)
                if s == QKV + 1:
                    dve.wait_ge(f_v4, b + 1)
                    values(NT, 1, 0).then_inc(s_v4, 1)
                if s == QKV + 2:
                    dve.wait_ge(s_v4, b + 1)
                    dve.tensor_copy(va[:, :, :, 0, 0:HD], heads_of(vf)).then_inc(s_vr, 1)
                if 0 <= w - 4 < NU:
                    if w >= 7:
                        dve.wait_ge(f_pv, NU * b + w - 6)
                    dve.wait_ge(s_pT, NU * b + w - 3)
                    dve.tensor_copy(pS[:, (w - 4) % 3, 0], pT[:, (w - 4) % 3]).then_inc(s_pr2, 1)
                t, hp = divmod(w - context_slot(b), NH // 2)
                if hp == NH // 2 - 1 and 0 <= t < NT:
                    dve.wait_ge(f_pv, NU * b + (t + 1) * NH // 2)
                    v = side[:, 2, 0:NH * VW].rearrange("p (h k e) -> p h e k", h=NH, k=2)
                    dve.tensor_reduce(vs[:, :, :], v, AX.X, ALU.add).then_inc(s_vs, 1)
                t, hp = divmod(w - context_slot(b) - 1, NH // 2)
                if hp == NH // 2 - 1 and 0 <= t < NT:
                    dve.wait_ge(s_vs, NT * b + t + 1)
                    link(dve.reciprocal(rd[:, :].unsqueeze(2), vs[:, :, HD:HD + 1]))
                    dve.tensor_tensor(cx[:, t, :].rearrange("p (h e) -> p h e", h=NH), vs[:, :, 0:HD],
                                      rd[:, :].unsqueeze(2).to_broadcast([P, NH, HD]), ALU.mult).then_inc(s_cx, 1)
                if s == PROJ:
                    dve.wait_ge(f_proj, b + 1)
                    dve.wait_ge(s_x2b, b + 1)
                    dve.tensor_tensor(x3[:, :, :], tiles(side[:, 1, :]), x2b[:, :, :], ALU.add).then_inc(s_x3, 1)
                if s in (LN4_A, LN4_A + 1):
                    if s == LN4_A:
                        dve.wait_ge(s_x3, b + 1)
                    norm_stats(3, x3, s - LN4_A)
                if s == FFN:
                    dve.wait_ge(f_ffn, b + 1)
                    dve.wait_ge(s_x3b, b + 1)
                    dve.tensor_tensor(osb[:, :, :], tiles(side[:, 2, :]), x3b[:, :, :], ALU.add).then_inc(s_o, 1)

            def values(m, bank, at):
                lo, hi = chunk_tokens(m)
                n = hi - lo
                return dve.scalar_tensor_tensor(vf[0:n, m, :], side[0:n, bank, at:at + P], WS, bvs[0:n, :],
                                                ALU.mult, ALU.add)

            def wait_scores(b, w):
                dve.wait_ge(f_sc, NU * b + w + 1)
                if w >= 3:
                    dve.wait_ge(f_pT, NU * b + w - 2)

            def masked(b, w):
                lo, hi, off = window(w // (NH // 2))
                n = hi - lo
                for k in range(2):
                    last = dve.tensor_tensor_reduce(sm[:, w % 3, k, off:off + n],
                                                    scores_bank(b, w)[:, k * WIN + off:k * WIN + off + n],
                                                    c["band"][:, off:off + n], -1.0 / HD ** 0.5, 3e38, ALU.add, ALU.min,
                                                    mn[:, w % 3, k:k + 1])
                last.then_inc(s_sm, 1)

            def gated(i, j):
                dve.wait_ge(s_u, NJ * i + j + 1)
                if j < NP:
                    dve.wait_ge(s_g, NP * i + j + 1)
                    dve.tensor_tensor(tb[:, j % 3, :], gp[:, j % 2, :], tb[:, j % 3, :], ALU.mult).then_inc(s_h, 1)
                else:
                    dve.tensor_scalar(tb[0:INTER, j % 3, :], tb[0:INTER, j % 3, :], 0.5 / WS, None,
                                      ALU.mult).then_inc(s_h, 1)

            def iteration(i, par, before, after, ahead):
                for s in range(NJ):
                    if before and 0 <= s - 1 - UNITS < NU:
                        wait_scores(i - 1, s - 1 - UNITS)
                    if s >= 1:
                        gated(i, s - 1)
                    elif before:
                        gated(i - 1, NJ - 1)
                    if before and 0 <= s - 1 - UNITS < NU:
                        masked(i - 1, s - 1 - UNITS)
                    n = P if s < NP else INTER
                    dve.wait_ge(s_t, NJ * i + s + 1)
                    dve.scalar_tensor_tensor(tb[0:n, s % 3, :], tb[0:n, s % 3, :], 1.0, zp[0:n, (par + s) % 2, :],
                                             ALU.add, ALU.mult).then_inc(s_u, 1)
                    if before:
                        banded(i - 1, 1 - par, s)
                    if not before:
                        take_up(1, s + LN1_A)
                        linear(1, s + LINEAR_1)
                        split_beside(s)
                    if after:
                        routing(i + 1, 1 - par, s, before)
                    if ahead:
                        take_up(i + 2, s if before else s - LN1_A_2)
                        linear(i + 2, s)
                if before:
                    dve.wait_ge(s_out, 16 * i)

            def prologue():
                setup()
                for s in range(NJ):
                    linear(0, s)
                    for n, slot in enumerate(EARLY_SPLITS):
                        if slot == s:
                            split(n)
                for s in range(NJ):
                    routing(0, 0, s, False)
                late_setup()

            def epilogue():
                gated(NB - 1, NJ - 1)
                for s in range(NJ):
                    if 0 <= s - UNITS < NU:
                        wait_scores(NB - 1, s - UNITS)
                        masked(NB - 1, s - UNITS)
                    banded(NB - 1, 1, s)

            run_batches(dve, prologue, iteration, epilogue)

        @block.gpsimd
        def _(pool):
            def rest(i, j):
                n = P if j < NP else INTER
                pool.wait_ge(s_hr, NJ * i + j + 1)
                pool.tensor_tensor(hh[0:n, j % 3, 1, :], tb[0:n, j % 3, :], hh[0:n, j % 3, 0, :],
                                   ALU.subtract).then_inc(s_hl, 1)

            def inverse_root(n, b):
                pool.wait_ge(s_var[n], b + 1)
                pool.tensor_tensor(ve[n][:, :].unsqueeze(2), mv[n][:, :, 1:2], a["eps"].unsqueeze(2), ALU.add)
                pool.tensor_tensor(minus[n][:, :].unsqueeze(2), mv[n][:, :, 0:1], a["mone"].unsqueeze(2), ALU.mult)
                pool.drain()
                pool.tensor_tensor(rstd[n][:, :], ve[n][:, :], a["mhalf"], ALU.pow)
                pool.drain()
                pool.tensor_tensor(shift[n][:, :], minus[n][:, :], rstd[n][:, :], ALU.mult).then_inc(s_rstd[n], 1)

            def take_up(b, s):
                if s == LN1_A + 2:
                    inverse_root(0, b)

            def linear(b, s):
                if s == LN2_A + 2:
                    inverse_root(1, b)

            def routing(b, s, before):
                for step in routing_steps(s, not before):
                    routing_step(b, step)

            def routing_step(b, s):
                if s == WEIGH:
                    pool.wait_ge(s_prob, 2 * NT * (b + 1))
                    pool.tensor_tensor(wt[:, :, :], prob[:, :, :], sel[:, :, :], ALU.mult).then_inc(s_wt, 1)

            def banded(b, s):
                bias = lambda n: c[n].unsqueeze(1).to_broadcast([P, NT, P])
                if s == LN3_A + 2:
                    inverse_root(2, b)
                if s == QKV + 5:
                    pool.tensor_tensor(x2b[:, :, :], x2[:, :, :], bias("bo"), ALU.add).then_inc(s_x2b, 1)
                if s == LN4_A + 2:
                    inverse_root(3, b)
                if s == LN4_B + 3:
                    pool.tensor_tensor(x3b[:, :, :], x3[:, :, :], bias("fbias"), ALU.add).then_inc(s_x3b, 1)
                if s == QKV + 3:
                    pool.wait_ge(s_vr, b + 1)
                    pool.tensor_tensor(va[:, :, :, 1, 0:HD], heads_of(vf), va[:, :, :, 0, 0:HD],
                                       ALU.subtract).then_inc(s_vl, 1)
                w = s - UNITS - 4
                if 0 <= w < NU:
                    pool.wait_ge(s_pr2, NU * b + w + 1)
                    pool.tensor_tensor(pS[:, w % 3, 1], pT[:, w % 3], pS[:, w % 3, 0], ALU.subtract).then_inc(s_pl, 1)

            def iteration(i, par, before, after, ahead):
                for s in range(NJ):
                    if s >= 1:
                        rest(i, s - 1)
                    elif before:
                        rest(i - 1, NJ - 1)
                    if before:
                        banded(i - 1, s)
                    if not before:
                        take_up(1, s + LN1_A)
                        linear(1, s + LINEAR_1)
                    if after:
                        routing(i + 1, s, before)
                    if ahead:
                        take_up(i + 2, s if before else s - LN1_A_2)
                        linear(i + 2, s)

            def prologue():
                pool.wait_ge(s_a, 16)
                for s in range(NJ):
                    take_up(0, s)
                for s in range(NJ):
                    linear(0, s)
                for s in range(NJ):
                    routing(0, s, False)
                pool.wait_ge(s_b, 16)

            def epilogue():
                rest(NB - 1, NJ - 1)
                for s in range(NJ):
                    banded(NB - 1, s)

            run_batches(pool, prologue, iteration, epilogue)


def packed(pack, parts):
    cols, width = columns(pack)
    out = np.zeros((P, width), np.float32)
    for name, (lo, hi) in cols.items():
        out[:parts[name].shape[0], lo:hi] = parts[name]
    return out


def stacked(q, k):
    out = np.zeros((q.shape[0], 2, NH, 32), np.float32)
    for n, v in enumerate((q, k)):
        for copy in range(3):
            out[:, n, :, copy * HD:(copy + 1) * HD] = v.reshape(-1, NH, HD)
    return out.reshape(q.shape[0], 8 * P)


def shape_constants():
    k = np.arange(P)
    angle = 2 * np.pi * ((k[:, None] * k[None, :]) % P) / P
    col = np.arange(WIN)
    part = (k % 32) // HD
    rest = np.stack([part == 2, part == 1], axis=1)
    spread = np.zeros((P, PPG * P), np.float32)
    for row in range(2 * GE):
        for_expert = row % GE
        spread[row, for_expert * INTER:(for_expert + 1) * INTER] = 1.0 / GS
    return {
        "ident": np.eye(P), "causal": (k[None, :] >= k[:, None]).astype(np.float32), "mhalf": np.full((P, NT), -0.5),
        "mone": np.full((P, NT), -1.0),
        "eps": np.full((P, NT), LN_EPS),
        "band": np.where((col[None, :] >= k[:, None]) & (col[None, :] <= k[:, None] + 2 * HALF), 0.0, -BIG),
        "rest": rest.astype(np.float32),
        "cos": np.cos(angle), "sin": np.sin(angle), "nsin": -np.sin(angle),
    }, spread


def kernel(L0_attn_hidden_states, L0_attn_w_q, L0_attn_w_k, L0_attn_w_v, L0_attn_w_o, L0_attn_gate, L0_attn_memory,
           L0_attn_memory_norm, L0_ffn_router_w, L0_ffn_expert_bias, L0_ffn_w_gate, L0_ffn_w_down,
           L0_ffn_w_gate_shared, L0_ffn_w_down_shared, L1_attn_Wq, L1_attn_bq, L1_attn_Wk, L1_attn_bk, L1_attn_Wv,
           L1_attn_bv, L1_attn_Wo, L1_attn_bo, L1_ffn_w_freq_real, L1_ffn_w_freq_imag, L1_ffn_bias):
    import concourse.bacc as bacc
    from concourse.bass_utils import run_bass_kernel_spmd

    const, spread = shape_constants()
    rows = lambda v, n=P: np.broadcast_to(np.asarray(v)[None, :], (n, np.asarray(v).shape[0]))
    T = lambda v: np.asarray(v).T
    col = lambda v: np.asarray(v)[:, None]
    bias2 = np.concatenate([np.asarray(L0_ffn_expert_bias)] * 2)
    in_a = packed(PACK_A, {
        **const, "wqk0": np.concatenate([T(L0_attn_w_q), T(L0_attn_w_k)], axis=1), "wv0": T(L0_attn_w_v),
        "router": T(L0_ffn_router_w), "ebias": rows(bias2), "gate": rows(L0_attn_gate),
        "wo0": T(L0_attn_w_o), "mem": np.asarray(L0_attn_memory),
        "norm": col(L0_attn_memory_norm), "normrow": rows(L0_attn_memory_norm)})
    wqk, bqk = stacked(T(L1_attn_Wq), T(L1_attn_Wk)), stacked(rows(L1_attn_bq, 1), rows(L1_attn_bk, 1))
    in_b = packed(PACK_B, {
        **const, "wqk": wqk, "bqk": bqk.reshape(8, P).T, "wv": T(L1_attn_Wv), "wo": T(L1_attn_Wo),
        "bv": rows(L1_attn_bv), "bo": rows(L1_attn_bo), "fbias": rows(L1_ffn_bias),
        "wgs": T(L0_ffn_w_gate_shared), "wds": T(L0_ffn_w_down_shared)})
    in_d = packed(PACK_D, {
        **const, "fr": np.asarray(L1_ffn_w_freq_real), "fi": np.asarray(L1_ffn_w_freq_imag)})
    in_c = np.concatenate([spread, np.eye(P, dtype=np.float32)], axis=1).astype(np.float16)
    up = np.ascontiguousarray(np.asarray(L0_ffn_w_gate).transpose(2, 0, 1).reshape(H, NE * INTER))
    down = np.ascontiguousarray(
        np.asarray(L0_ffn_w_down).reshape(NP, 2, H, INTER).transpose(1, 3, 0, 2).reshape(P, NP * H))

    nc = bacc.Bacc("TRN2", target_bir_lowering=False, num_devices=1)
    arrays = {"in_x": np.ascontiguousarray(L0_attn_hidden_states), "in_a": in_a, "in_b": in_b, "in_c": in_c,
              "in_d": in_d, "in_up": up, "in_down": down}
    aps = [nc.dram_tensor(n, v.shape, mybir.dt.from_np(v.dtype), kind="ExternalInput").ap() for n, v in arrays.items()]
    out = nc.dram_tensor("out_y", (NB, SEQ, H), F32, kind="ExternalOutput").ap()
    build(nc, *aps, out)
    r = run_bass_kernel_spmd(nc, [arrays], core_ids=[0])
    return r.results[0]["out_y"]
```
